# Optimizing a Trainium2 kernel written in Bass

```python
import numpy as np
import jax
import jax.numpy as jnp

def _softmax(x, axis=-1):
    return jax.nn.softmax(x, axis=axis)

def _gelu(x):
    return jax.nn.gelu(x, approximate=True)

def _silu(x):
    return jax.nn.silu(x)

def _sigmoid(x):
    return jax.nn.sigmoid(x)

def _layernorm(x, axis=-1, eps=1e-05):
    m = jnp.mean(x, axis=axis, keepdims=True)
    v = jnp.var(x, axis=axis, keepdims=True)
    return (x - m) / jnp.sqrt(v + eps)

def _scatter_add(tgt, idx, src, axis=0):
    return tgt.at[idx].add(src)

def _segment_sum(src, seg, n):
    return jax.ops.segment_sum(src, seg, n)
kernel_name = 'mk_seq_preln_d1_jaxref_r8_355e80'

def setup_inputs(seed: int=0):
    np.random.seed(seed)
    _w = jnp.asarray

    def _L0_attn_setup():
        import jax, jax.numpy as jnp
        import numpy as np
        D_MODEL = 128
        N_HEADS = 16
        D_K = D_MODEL // N_HEADS
        IDX_HEADS = 4
        IDX_DIM = 64
        TOP_K = 64
        ROPE_BASE = 1250
        NEG_INF = -1e+30

        def _rope(x):
            b, s, h, d = x.shape
            inv_freq = 1.0 / ROPE_BASE ** (jnp.arange(0, d, 2, dtype=jnp.float32) / d)
            t = jnp.arange(s, dtype=jnp.float32)
            freqs = jnp.outer(t, inv_freq)
            cos = jnp.cos(freqs)[None, :, None, :]
            sin = jnp.sin(freqs)[None, :, None, :]
            x1, x2 = (x[..., ::2], x[..., 1::2])
            o1 = x1 * cos - x2 * sin
            o2 = x2 * cos + x1 * sin
            return jnp.stack([o1, o2], axis=-1).reshape(b, s, h, d).astype(x.dtype)
        key = jax.random.key(seed)
        ks = jax.random.split(key, 6)
        B, S, D = (2, 256, D_MODEL)
        sd = 1.0 / np.sqrt(D)
        return {'x': jax.random.normal(ks[0], (B, S, D), jnp.float32), 'qkv_w': jax.random.uniform(ks[1], (3 * D, D), jnp.float32, -sd, sd), 'wo_w': jax.random.uniform(ks[2], (D, D), jnp.float32, -sd, sd), 'iq_w': jax.random.uniform(ks[3], (IDX_HEADS * IDX_DIM, D), jnp.float32, -sd, sd), 'ik_w': jax.random.uniform(ks[4], (IDX_DIM, D), jnp.float32, -sd, sd), 'iw_w': jax.random.uniform(ks[5], (IDX_HEADS, D), jnp.float32, -sd, sd)}
    _L0_attn_in = _L0_attn_setup()

    def _L0_ffn_setup():
        import jax, jax.numpy as jnp
        import numpy as np
        N_EMBD = 128
        N_STATE = 512
        key = jax.random.key(seed)
        k_x, k_w1, k_b1, k_w2, k_b2 = jax.random.split(key, 5)
        x = jax.random.normal(k_x, (4, 256, N_EMBD), dtype=jnp.float32)
        w1 = jax.random.normal(k_w1, (N_EMBD, N_STATE), dtype=jnp.float32) * (1.0 / np.sqrt(N_EMBD))
        b1 = jax.random.normal(k_b1, (N_STATE,), dtype=jnp.float32) * 0.02
        w2 = jax.random.normal(k_w2, (N_STATE, N_EMBD), dtype=jnp.float32) * (1.0 / np.sqrt(N_STATE))
        b2 = jax.random.normal(k_b2, (N_EMBD,), dtype=jnp.float32) * 0.02
        return {'x': x, 'w1': w1, 'b1': b1, 'w2': w2, 'b2': b2}
    _L0_ffn_in = _L0_ffn_setup()
    _d = {'L0_attn_x': _L0_attn_in['x'], 'L0_attn_qkv_w': _L0_attn_in['qkv_w'], 'L0_attn_wo_w': _L0_attn_in['wo_w'], 'L0_attn_iq_w': _L0_attn_in['iq_w'], 'L0_attn_ik_w': _L0_attn_in['ik_w'], 'L0_attn_iw_w': _L0_attn_in['iw_w'], 'L0_ffn_w1': _L0_ffn_in['w1'], 'L0_ffn_b1': _L0_ffn_in['b1'], 'L0_ffn_w2': _L0_ffn_in['w2'], 'L0_ffn_b2': _L0_ffn_in['b2']}
    _x0 = _d['L0_attn_x']
    _d['L0_attn_x'] = jax.random.normal(jax.random.fold_in(jax.random.key(seed), 1), (4, 1024, 128), dtype=_x0.dtype)
    del _x0
    return _d

def reference(L0_attn_x, L0_attn_qkv_w, L0_attn_wo_w, L0_attn_iq_w, L0_attn_ik_w, L0_attn_iw_w, L0_ffn_w1, L0_ffn_b1, L0_ffn_w2, L0_ffn_b2):

    def _L0_attn_ref(x, qkv_w, wo_w, iq_w, ik_w, iw_w):
        import jax, jax.numpy as jnp
        import numpy as np
        D_MODEL = 128
        N_HEADS = 16
        D_K = D_MODEL // N_HEADS
        IDX_HEADS = 4
        IDX_DIM = 64
        TOP_K = 64
        ROPE_BASE = 1250
        NEG_INF = -1e+30

        def _rope(x):
            b, s, h, d = x.shape
            inv_freq = 1.0 / ROPE_BASE ** (jnp.arange(0, d, 2, dtype=jnp.float32) / d)
            t = jnp.arange(s, dtype=jnp.float32)
            freqs = jnp.outer(t, inv_freq)
            cos = jnp.cos(freqs)[None, :, None, :]
            sin = jnp.sin(freqs)[None, :, None, :]
            x1, x2 = (x[..., ::2], x[..., 1::2])
            o1 = x1 * cos - x2 * sin
            o2 = x2 * cos + x1 * sin
            return jnp.stack([o1, o2], axis=-1).reshape(b, s, h, d).astype(x.dtype)
        B, S, D = x.shape
        qkv = (x @ qkv_w.T).reshape(B, S, 3, N_HEADS, D_K).transpose(2, 0, 3, 1, 4)
        Q, K, V = (qkv[0], qkv[1], qkv[2])
        Q = _rope(Q.transpose(0, 2, 1, 3)).transpose(0, 2, 1, 3)
        K = _rope(K.transpose(0, 2, 1, 3)).transpose(0, 2, 1, 3)
        iq = (x @ iq_w.T).reshape(B, S, IDX_HEADS, IDX_DIM)
        ik = x @ ik_w.T
        iw = x @ iw_w.T
        dots = jnp.einsum('bthd,bsd->bths', iq, ik)
        index_scores = jnp.sum(jax.nn.relu(dots) * iw[..., None], axis=2)
        causal = jnp.triu(jnp.ones((S, S), jnp.bool_), 1)
        masked_scores = jnp.where(causal[None], -1000000000.0, index_scores)
        _, top_idx = jax.lax.top_k(masked_scores, TOP_K)
        top_mask = jnp.zeros((B, S, S), jnp.bool_).at[jnp.arange(B)[:, None, None], jnp.arange(S)[None, :, None], top_idx].set(True)
        bias = jnp.where(top_mask[:, None], 0.0, NEG_INF)
        logits = jnp.einsum('bhtd,bhsd->bhts', Q, K) / jnp.sqrt(jnp.float32(D_K)) + bias
        attn = jax.nn.softmax(logits, axis=-1)
        out = jnp.einsum('bhts,bhsd->bhtd', attn, V)
        out = out.transpose(0, 2, 1, 3).reshape(B, S, D)
        return out @ wo_w.T

    def _L0_ffn_ref(x, w1, b1, w2, b2):
        import jax, jax.numpy as jnp
        import numpy as np
        N_EMBD = 128
        N_STATE = 512
        h = jax.nn.gelu(jnp.einsum('bse,eh->bsh', x, w1) + b1, approximate=False)
        return jnp.einsum('bsh,he->bse', h, w2) + b2
    x = L0_attn_x
    x = x + _L0_attn_ref(_layernorm(x, axis=-1), L0_attn_qkv_w, L0_attn_wo_w, L0_attn_iq_w, L0_attn_ik_w, L0_attn_iw_w)
    x = x + _L0_ffn_ref(_layernorm(x, axis=-1), L0_ffn_w1, L0_ffn_b1, L0_ffn_w2, L0_ffn_b2)
    return x

_drawn_inputs = setup_inputs


def setup_inputs(seed=0):
    import zlib

    import numpy as np

    out = dict(_drawn_inputs(seed))
    spreads = {}
    factors = {'L0_ffn_b1': 5.116, 'L0_ffn_b2': 3.331}
    for name, (base, spread) in spreads.items():
        noise = np.random.default_rng([zlib.crc32(name.encode()), seed]).standard_normal(out[name].shape)
        drawn = base * np.exp(spread * noise) if base else spread * noise
        out[name] = jnp.asarray(drawn.astype(out[name].dtype))
    for name, factor in factors.items():
        out[name] = (out[name] * factor).astype(out[name].dtype)
    return out
```

```python
from contextlib import ExitStack

import concourse.bass as bass
from concourse import mybir

F32 = mybir.dt.float32
BF16 = mybir.dt.bfloat16
ALU = mybir.AluOpType
ACT = mybir.ActivationFunctionType
AX = mybir.AxisListType

P = 128
BANK = 512
B, S, D = 4, 1024, 128
HEADS, DK = 16, 8
IH, ID = 4, 64
TOPK = 64
STATE = 512
HG, HL = 4, 4
TILES = S // P
GROUPS = S // BANK
PARTS = 3
KROWS = PARTS * PARTS * DK
KC = KROWS + PARTS
VW = 32
EPS = 1e-5
NOT_CAUSAL = -1.0e9
TAKEN = -3.0e38
HIDE = -1.0e30
LOGIT_SCALE = float(DK) ** -0.5

STEPS = [(hg, g, j) for hg in range(HG) for g in range(GROUPS) for j in range(4 * g + 4)]
CHUNKS = [(i, c, min(BANK, P * (i + 1) - c), h)
          for i in range(TILES) for c in range(0, P * (i + 1), BANK) for h in range(IH)]
NSTEP, NCHUNK, NPAIR = len(STEPS), len(CHUNKS), 2 * len(STEPS)
assert NSTEP == NCHUNK == 48
NGRP = HG * GROUPS
HALF_CHUNKS = 16
GROUP_END = [k for k in range(NSTEP) if k + 1 == NSTEP or STEPS[k + 1][:2] != STEPS[k][:2]]
VECTOR_ORDER = [
    [("tile", 0), ("norm", 0), ("tile", 1), ("tile", 2), ("norm", 1)],
    [("tile", 3), ("norm", 2), ("tile", 4), ("norm", 3)],
    [("norm", 4), ("tile", 5), ("norm", 5)],
    [("norm", 6), ("tile", 6), ("tile", 7), ("norm", 7)],
]
QK_DMAS = 3 + 5
INDEX_DMAS = 6 + 4


def span(k):
    _, g, j = STEPS[k]
    t0 = max(P * j, BANK * g)
    return t0, BANK * (g + 1) - t0


def chain_on(eng, sem):
    count = [0]

    def link(ins):
        count[0] += 1
        ins.then_inc(sem, 1)
        eng.wait_ge(sem, count[0])

    def restart():
        count[0] = 0
        eng.sem_clear(sem)

    def step():
        count[0] += 1
        eng.sem_inc(sem, 1)
        eng.wait_ge(sem, count[0])

    return link, restart, step


def project_all(nc, t, v_all, iw_all):
    with ExitStack() as ctx:
        def sb(name, shape, dt):
            return ctx.enter_context(nc.sbuf_tensor(name, shape, dt))

        def sem(name):
            return ctx.enter_context(nc.semaphore(name))

        NT = BANK // P
        NW = 7 * P + IH
        COL = dict(q=0, qs=P, k=2 * P, ks=3 * P, iq0=4 * P, iq1=5 * P, ik=6 * P, v=6 * P + ID)
        w = sb("w", [P, NW + ID], F32)
        cos = sb("cos", [P, S], F32)
        sin = sb("sin", [P, S], F32)
        ident = sb("identA", [P, P], F32)
        xs = sb("xs", [P, 2, NT, D], F32)
        stats = sb("stats", [P, NT, 6], F32)
        mv = sb("mv", [P, NT, 2], F32)
        std = sb("std", [P, NT], F32)
        rstd = sb("rstd", [P, NT], F32)
        xn = sb("xn", [P, NT, D], F32)
        xT = sb("xT", [P, 2, BANK], F32)
        tc_ = sb("rope_cos", [P, 2, BANK], F32)
        ts_ = sb("rope_sin", [P, 2, BANK], F32)
        rot = sb("rot", [P, 2, BANK], F32)
        rest = sb("rest", [P, 2, BANK], F32)
        parts = sb("parts", [P, 5, PARTS, BANK], BF16)
        psx = ctx.enter_context(nc.psum_tensor("psx", [P, 8, BANK], F32))

        s_w = sem("weights_loaded")
        s_x = [sem(f"x_loaded{h}") for h in range(2)]
        s_bn = sem("moments_ready")
        s_std = sem("std_ready")
        s_xn = sem("xn_ready")
        s_t = sem("xn_turned")
        s_xT = sem("xT_copied")
        s_mm = sem("projected")
        s_rc = sem("rope_products")
        s_rot = sem("rotated")
        s_hi = sem("high_parts")
        s_r = sem("rests_ready")
        s_mid = sem("middle_parts")
        s_lo = sem("low_parts")
        s_st = sem("operands_stored")
        s_v = sem("values_copied")
        s_ch = sem("vector_chain_a")
        block = ctx.enter_context(nc.Block())

        PROD = [("q", 1), ("qs", 2), ("k", 3), ("ks", 4), ("iq0", 5), ("iq1", 6), ("ik", 7)]
        ORDER = ["q", "k", "iq0", "iq1", "ik"]
        NPROD = len(PROD) + 2

        @block.sync
        def _(sp):
            sp.dma_start(w[:], t["w"]).then_inc(s_w, 16)
            sp.dma_start(cos[:], t["cos"]).then_inc(s_w, 16)
            sp.dma_start(sin[:], t["sin"]).then_inc(s_w, 16)
            sp.dma_start(ident[:], t["ident"]).then_inc(s_w, 16)

            def load(b, half):
                sp.dma_start(xs[:, half], t["x"][b, half]).then_inc(s_x[half], 16)

            load(0, 0)
            load(0, 1)

            def batch(b, more):
                for half in range(2):
                    n = 2 * b + half
                    for a, name in enumerate(ORDER):
                        sp.wait_ge(s_mid, 5 * n + a + 1)
                        sp.wait_ge(s_lo, 5 * n + a + 1)
                        rows = ID if name == "ik" else P
                        src = parts[0:rows, a]
                        cols = slice(half * BANK, (half + 1) * BANK)
                        sp.dma_start(t[name + "_parts"][b, :, :, cols].rearrange("p c t -> c p t"),
                                     src).then_inc(s_st, 16)
                    if more:
                        sp.wait_ge(s_xn, n + 1)
                        load(b + 1, half)

            with sp.Fori(0, B - 1) as b:
                batch(b, True)
            batch(B - 1, False)
            sp.wait_ge(s_st, 16 * 5 * 2 * B)

        @block.vector
        def _(dve):
            link, restart, _ = chain_on(dve, s_ch)
            with dve.Fori(0, B) as b:
                for half in range(2):
                    n = 2 * b + half
                    x = xs[:, half]
                    dve.wait_ge(s_x[half], 16 * b + 16)
                    for j in range(NT):
                        last = nc.vector.bn_stats(stats[:, j], x[:, j])
                        link(last)
                    for j in range(NT):
                        last = nc.vector.bn_aggr(mv[:, j], stats[:, j])
                        if j < NT - 1:
                            link(last)
                    last.then_inc(s_bn, 1)
                    dve.wait_ge(s_std, n + 1)
                    link(nc.vector.reciprocal(rstd[:], std[:]))
                    if half:
                        dve.wait_ge(s_t, n)
                    else:
                        dve.wait_ge(s_t, n)
                    for j in range(NT):
                        last = nc.vector.tensor_scalar(xn[:, j], x[:, j], mv[:, j, 0:1], rstd[:, j:j + 1],
                                                       ALU.subtract, ALU.mult)
                    last.then_inc(s_xn, 1)
                    cols = slice(half * BANK, (half + 1) * BANK)
                    for a in range(2):
                        dve.wait_ge(s_mm, NPROD * n + 2 * a + 2)
                        dve.wait_ge(s_rot, 2 * n + a)
                        if a == 0:
                            dve.wait_ge(s_w, 64)
                        nc.vector.tensor_tensor(tc_[:, a], psx[:, 1 + 2 * a], cos[:, cols], ALU.mult)
                        nc.vector.tensor_tensor(ts_[:, a], psx[:, 2 + 2 * a], sin[:, cols],
                                                ALU.mult).then_inc(s_rc, 1)
                    for a, name in enumerate(ORDER):
                        rows = ID if name == "ik" else P
                        src = rot[0:rows, a] if a < 2 else psx[0:rows, 3 + a]
                        dve.wait_ge(s_lo, 5 * n + a - 1) if not (a < 1) else dve.wait_ge(s_lo, 5 * n)
                        dve.wait_ge(s_hi, 5 * n + a + 1)
                        nc.vector.tensor_tensor(rest[0:rows, a % 2], src, parts[0:rows, a, 0],
                                                ALU.subtract).then_inc(s_r, 1)
                    restart()

        @block.scalar
        def _(act):
            with act.Fori(0, B) as b:
                for half in range(2):
                    n = 2 * b + half
                    act.wait_ge(s_w, 64)
                    act.wait_ge(s_bn, n + 1)
                    nc.scalar.activation(std[:], mv[:, :, 1], ACT.Sqrt, bias=EPS).then_inc(s_std, 1)
                    act.wait_ge(s_mm, NPROD * n)
                    act.wait_ge(s_t, n + 1)
                    nc.scalar.copy(xT[:, half], psx[:, 0]).then_inc(s_xT, 1)
                    for a, name in enumerate(ORDER):
                        rows = ID if name == "ik" else P
                        src = rot[0:rows, a] if a < 2 else psx[0:rows, 3 + a]
                        act.wait_ge(s_st, 16 * 5 * n)
                        if a < 2:
                            act.wait_ge(s_rot, 2 * n + a + 1)
                        else:
                            act.wait_ge(s_mm, NPROD * n + 3 + a)
                        nc.scalar.copy(parts[0:rows, a, 0], src).then_inc(s_hi, 1)
                        act.wait_ge(s_r, 5 * n + a + 1)
                        nc.scalar.copy(parts[0:rows, a, 1], rest[0:rows, a % 2]).then_inc(s_mid, 1)
                    for e in range(2):
                        act.wait_ge(s_mm, NPROD * n + 8 + e)
                        src = psx[:, e, 0:2 * (P + IH)].rearrange("p (j c) -> p j c", j=2)
                        tile = NT * n + 2 * e
                        nc.scalar.copy(v_all[:, bass.ds(tile, 2), :], src[:, :, 0:P])
                        nc.scalar.copy(iw_all[:, bass.ds(tile, 2), :], src[:, :, P:P + IH]).then_inc(s_v, 1)

        @block.gpsimd
        def _(pool):
            with pool.Fori(0, B) as b:
                for half in range(2):
                    n = 2 * b + half
                    for a in range(2):
                        pool.wait_ge(s_r, 5 * n)
                        pool.wait_ge(s_hi, 5 * n)
                        pool.wait_ge(s_rc, 2 * n + a + 1)
                        nc.gpsimd.tensor_tensor(rot[:, a], tc_[:, a], ts_[:, a], ALU.add).then_inc(s_rot, 1)
                    for a, name in enumerate(ORDER):
                        rows = ID if name == "ik" else P
                        pool.wait_ge(s_mid, 5 * n + a + 1)
                        nc.gpsimd.tensor_tensor(parts[0:rows, a, 2], rest[0:rows, a % 2],
                                                parts[0:rows, a, 1], ALU.subtract).then_inc(s_lo, 1)

        @block.tensor
        def _(pe):
            with pe.Fori(0, B) as b:
                for half in range(2):
                    n = 2 * b + half
                    pe.wait_ge(s_v, 2 * n)
                    pe.wait_ge(s_w, 64)
                    pe.wait_ge(s_xn, n + 1)
                    for j in range(NT):
                        last = nc.tensor.transpose(psx[:, 0, P * j:P * (j + 1)], xn[:, j], ident[:])
                    last.then_inc(s_t, 1)
                    pe.wait_ge(s_xT, n + 1)
                    for a, (name, bank) in enumerate(PROD):
                        rows = ID if name == "ik" else P
                        if a < 4:
                            pe.wait_ge(s_rc, 2 * n)
                            pe.wait_ge(s_v, 2 * n)
                        else:
                            pe.wait_ge(s_hi, 5 * n)
                            pe.wait_ge(s_r, 5 * n)
                        nc.tensor.matmul(psx[0:rows, bank], w[:, COL[name]:COL[name] + rows], xT[:, half],
                                         start=True, stop=True).then_inc(s_mm, 1)
                    for e in range(2):
                        if e == 1:
                            pe.wait_ge(s_rc, 2 * n + 1)
                        for j in range(2):
                            tile = 2 * e + j
                            last = nc.tensor.matmul(psx[:, e, (P + IH) * j:(P + IH) * (j + 1)],
                                                    xT[:, half, P * tile:P * (tile + 1)],
                                                    w[:, COL["v"]:COL["v"] + P + IH], start=True, stop=True)
                        last.then_inc(s_mm, 1)


def attend_all(nc, t, v_all, iw_all):
    with ExitStack() as ctx:
        def sb(name, shape, dt):
            return ctx.enter_context(nc.sbuf_tensor(name, shape, dt))

        def sem(name):
            return ctx.enter_context(nc.semaphore(name))

        ident = sb("ident", [P, P], F32)
        identb = sb("identb", [P, P], BF16)
        q_op = sb("q_op", [KC, 2, HL, S], BF16)
        k_op = sb("k_op", [KC, 2, HL, S], BF16)
        v_op = sb("v_op", [P, TILES, HEADS, VW], F32)
        iq_op = sb("iq_op", [P, 2, 3, IH, BANK], BF16)
        ik_op = sb("ik_op", [P, 2, 2, S], BF16)
        iw_cur = sb("iw_cur", [P, TILES, IH], F32)
        hidden = sb("hidden", [P, TILES, S], BF16)
        hidden_t = sb("hidden_t", [P, TILES, S], BF16)
        probs = sb("probs", [P, 2, HL, BANK], F32)
        relu = sb("relu", [P, 4, BANK], F32)
        index = sb("index", [P, 2, S], F32)
        best = sb("best", [P, 8], F32)
        out_t = sb("out_t", [P, 2, BANK], F32)
        recip = sb("recip", [P, 4, HL], F32)
        rows_out = sb("rows_out", [P, TILES, D], F32)
        top = sb("top", [P, TILES * HL], F32)
        neg = sb("neg", [TILES * HL, 3, P], F32)
        neg_parts = sb("neg_parts", [TILES * HL, PARTS, P], BF16)

        ps_s = ctx.enter_context(nc.psum_tensor("ps_s", [P, 4, BANK], F32))
        ps_o = ctx.enter_context(nc.psum_tensor("ps_o", [P, BANK], F32))
        ps_d = ctx.enter_context(nc.psum_tensor("ps_d", [P, 2, BANK], F32))
        ps_t = ctx.enter_context(nc.psum_tensor("ps_t", [P, BANK], F32))
        turn_banks = [ps_t[:].bitcast(BF16), ps_d[:, 0].bitcast(BF16)]

        s_id = sem("identities_loaded")
        s_init = sem("operands_filled")
        s_qk = [sem(f"qk_loaded{r}") for r in range(2)]
        s_iqk = [sem(f"index_operands_loaded{r}") for r in range(2)]
        s_dots = sem("dots_ready")
        s_relu = sem("relu_ready")
        s_relu_used = sem("relu_used")
        s_index = sem("index_ready")
        s_sel = sem("selected")
        s_turned = sem("selection_turned")
        s_hid = sem("hidden_t_ready")
        s_v = sem("values_placed")
        s_sc = sem("logits_ready")
        s_p = sem("probs_ready")
        s_pv = sem("pv_done")
        s_oc = sem("out_copied")
        s_ot = sem("out_turned")
        s_norm = sem("normalised")
        s_ms = sem("max_logits_ready")
        s_mt = sem("max_taken")
        s_mtop = sem("maxima_ready")
        s_mturn = sem("maxima_turned")
        s_neg = sem("neg_parts_ready")
        s_cl = sem("max_rows_loaded")
        s_st = sem("rows_stored")
        s_chv = sem("vector_chain")
        s_chp = sem("pool_chain")
        block = ctx.enter_context(nc.Block())

        NMAX = TILES * HL

        @block.sync
        def _(sp):
            sp.dma_start(ident[:], t["ident"]).then_inc(s_id, 16)
            sp.dma_start(identb[:], t["identb"]).then_inc(s_id, 16)

            def load_qk(b, hg):
                r = hg % 2
                rows = slice(32 * hg, 32 * hg + 32)
                q = t["q_parts"][b, :, rows, :].rearrange("p (d h) t -> p d (h t)", h=HL)
                k = t["k_parts"][b, :, rows, :].rearrange("p (d h) t -> p d (h t)", h=HL)
                G = PARTS * DK
                for rep in range(PARTS):
                    sp.dma_start(q_op[G * rep:G * rep + G, r].rearrange("p h t -> p (h t)"), q)\
                      .then_inc(s_qk[r], 16)
                    cut = DK * (PARTS - rep)
                    sp.dma_start(k_op[G * rep:G * rep + cut, r].rearrange("p h t -> p (h t)"), k[rep:])\
                      .then_inc(s_qk[r], 16)
                    if rep:
                        sp.dma_start(k_op[G * rep + cut:G * rep + G, r].rearrange("p h t -> p (h t)"), k[:rep])\
                          .then_inc(s_qk[r], 16)

            def load_index(b, half):
                n = BANK * (half + 1)
                for combo, pair in enumerate(((0, 0), (1, 1), (0, 2))):
                    for lo, part in enumerate(pair):
                        src = [t["iq0_parts"], t["iq1_parts"]]
                        for e in range(2):
                            sp.dma_start(
                                iq_op[ID * lo:ID * lo + ID, half, combo, 2 * e:2 * e + 2],
                                src[e][b, part, :, BANK * half:BANK * (half + 1)].rearrange("(h d) t -> d h t", h=2)
                            ).then_inc(s_iqk[half], 16)
                for combo, pair in enumerate(((0, 1), (2, 0))):
                    for lo, part in enumerate(pair):
                        sp.dma_start(ik_op[ID * lo:ID * lo + ID, half, combo, 0:n],
                                     t["ik_parts"][b, part, :, 0:n]).then_inc(s_iqk[half], 16)

            def load_maxima(b, hg):
                sp.wait_ge(s_neg, HG * b + hg + 1)
                for p in range(PARTS):
                    dst = q_op[KROWS + p:KROWS + p + 1, hg % 2].rearrange("o h (i t) -> o (h i) t", i=TILES)
                    sp.dma_start(dst, neg_parts[:, p, :]).then_inc(s_cl, 16)

            load_index(0, 0)
            load_index(0, 1)
            sp.wait_ge(s_init, 1)
            load_qk(0, 0)
            load_qk(0, 1)

            def batch(b, more):
                if more:
                    sp.wait_ge(s_dots, NCHUNK * b + NCHUNK)
                    load_index(b + 1, 0)
                    load_index(b + 1, 1)
                for hg in range(HG):
                    load_maxima(b, hg)
                    if hg + 2 < HG or more:
                        sp.wait_ge(s_sc, NPAIR * b + (NPAIR // HG) * (hg + 1))
                        load_qk(b + (hg + 2) // HG, (hg + 2) % HG)

            with sp.Fori(0, B - 1) as b:
                batch(b, True)
            batch(B - 1, False)
            sp.wait_ge(s_st, 16 * B)

        @block.tensor
        def _(pe):
            def dots(n, c):
                i, c0, wd, h = CHUNKS[c]
                half = i // 4
                if c == 0:
                    pe.wait_ge(s_iqk[0], 16 * 16 * n + 256)
                if c == HALF_CHUNKS:
                    pe.wait_ge(s_iqk[1], 16 * 16 * n + 256)
                if c >= 2 or not isinstance(n, int):
                    pe.wait_ge(s_relu, NCHUNK * n + c - 1)
                qc = slice(P * (i % 4), P * (i % 4) + P)
                for m, kc in enumerate((0, 0, 1)):
                    last = nc.tensor.matmul(ps_d[:, c % 2, 0:wd], iq_op[:, half, m, h, qc],
                                            ik_op[:, half, kc, c0:c0 + wd], start=(m == 0), stop=(m == 2))
                last.then_inc(s_dots, 1)

            def turn_selection(b):
                pe.wait_ge(s_sel, TILES * b + TILES)
                pe.wait_ge(s_relu, NCHUNK * b + NCHUNK)
                if not (isinstance(b, int) and b == 0):
                    pe.wait_ge(s_norm, NGRP * b)
                for j in range(TILES):
                    if j >= 2:
                        pe.wait_ge(s_hid, TILES * b + j - 1)
                    for i in range(j, TILES):
                        last = nc.tensor.transpose(turn_banks[j % 2][:, P * (i - j):P * (i - j + 1)],
                                                   hidden[:, i, P * j:P * (j + 1)], identb[:])
                    last.then_inc(s_turned, 1)

            def row_maxima(b, hg):
                r = hg % 2
                pe.wait_ge(s_qk[r], 16 * QK_DMAS * (2 * b + hg // 2 + 1))
                pe.wait_ge(s_p, NPAIR * b + (NPAIR // HG) * hg)
                for m in range(NMAX):
                    i, hl = m // HL, m % HL
                    if m >= 2:
                        pe.wait_ge(s_mt, NMAX * (HG * b + hg) + m - 1)
                    for c0 in range(0, P * (i + 1), BANK):
                        wd = min(BANK, P * (i + 1) - c0)
                        bank = ps_s[:, 2 * (m % 2) + c0 // BANK, 0:wd]
                        nc.tensor.matmul(bank, q_op[0:KROWS, r, hl, P * i:P * (i + 1)],
                                         k_op[0:KROWS, r, hl, c0:c0 + wd], start=True, stop=False,
                                         skip_group_check=True)
                        for j in range(c0 // P, (c0 + wd) // P):
                            last = nc.tensor.matmul(bank[:, P * j - c0:P * j - c0 + P],
                                                    hidden_t[:, j, P * i:P * (i + 1)], identb[:],
                                                    start=False, stop=(P * (j + 1) == c0 + wd),
                                                    skip_group_check=True)
                    last.then_inc(s_ms, 1)
                pe.wait_ge(s_mtop, HG * b + hg + 1)
                if not (isinstance(b, int) and b == 0 and hg == 0):
                    pe.wait_ge(s_norm, NGRP * b + 2 * hg)
                nc.tensor.transpose(ps_t[0:NMAX, 0:P], top[:], ident[:]).then_inc(s_mturn, 1)

            def logits(b, k):
                hg, g, j = STEPS[k]
                r = hg % 2
                t0, wd = span(k)
                if k == 0 or STEPS[k - 1][0] != hg:
                    pe.wait_ge(s_cl, 16 * PARTS * (HG * b + hg + 1))
                for p in range(2):
                    if k or p:
                        if 2 * k + p >= 2:
                            pe.wait_ge(s_p, NPAIR * b + 2 * k + p - 1)
                    for e in range(2):
                        nc.tensor.matmul(ps_s[:, 2 * p + e, 0:wd], identb[:], hidden_t[:, j, t0:t0 + wd],
                                         start=True, stop=False)
                    for e in range(2):
                        last = nc.tensor.matmul(ps_s[:, 2 * p + e, 0:wd], k_op[:, r, 2 * p + e, P * j:P * (j + 1)],
                                                q_op[:, r, 2 * p + e, t0:t0 + wd], start=False, stop=True)
                    last.then_inc(s_sc, 1)

            def weigh(b, k):
                hg, g, j = STEPS[k]
                t0, wd = span(k)
                n = GROUPS * hg + g
                if k == 0:
                    pe.wait_ge(s_v, b + 1)
                if j == 0 and not (isinstance(b, int) and b == 0 and n == 0):
                    pe.wait_ge(s_oc, NGRP * b + n)
                pe.wait_ge(s_p, NPAIR * b + 2 * k + 2)
                for hl in range(HL):
                    last = nc.tensor.matmul(ps_o[VW * hl:VW * (hl + 1), t0 - BANK * g:BANK],
                                            v_op[:, j, HL * hg + hl, :], probs[:, k % 2, hl, 0:wd],
                                            start=(j == 0), stop=(k in GROUP_END))
                last.then_inc(s_pv, 1)

            def turn_out(b, n):
                pe.wait_ge(s_oc, NGRP * b + n + 1)
                if n:
                    pe.wait_ge(s_norm, NGRP * b + n)
                for c in range(4):
                    last = nc.tensor.transpose(ps_t[:, P * c:P * (c + 1)], out_t[:, n % 2, P * c:P * (c + 1)],
                                               ident[:])
                last.then_inc(s_ot, 1)

            def batch(b, more):
                turn_selection(b)
                pe.wait_ge(s_hid, TILES * b + TILES)
                for k in range(NSTEP):
                    hg, g, j = STEPS[k]
                    first = g == 0 and j == 0
                    if first:
                        row_maxima(b, hg)
                        logits(b, k)
                    if k + 1 < NSTEP and STEPS[k + 1][0] == hg:
                        logits(b, k + 1)
                    weigh(b, k)
                    if k - 1 in GROUP_END and STEPS[k][0] == STEPS[k - 1][0]:
                        turn_out(b, GROUP_END.index(k - 1))
                    if more:
                        dots(b + 1, k)
                    if k in GROUP_END and (k + 1 == NSTEP or STEPS[k + 1][0] != hg):
                        turn_out(b, GROUP_END.index(k))

            pe.wait_ge(s_id, 32)
            for c in range(NCHUNK):
                dots(0, c)
            with pe.Fori(0, B - 1) as b:
                batch(b, True)
            batch(B - 1, False)

        @block.scalar
        def _(act):
            def keep_positive(n, c):
                i, c0, wd, h = CHUNKS[c]
                act.wait_ge(s_dots, NCHUNK * n + c + 1)
                if c >= 4 or not isinstance(n, int):
                    act.wait_ge(s_relu_used, NCHUNK * n + c - 3)
                nc.scalar.activation(relu[:, c % 4, 0:wd], ps_d[:, c % 2, 0:wd], ACT.Relu).then_inc(s_relu, 1)

            def exponents(b, k):
                t0, wd = span(k)
                act.wait_ge(s_pv, NSTEP * b + max(k - 1, 0))
                for p in range(2):
                    act.wait_ge(s_sc, NPAIR * b + 2 * k + p + 1)
                    nc.scalar.activation(probs[:, k % 2, 2 * p:2 * p + 2, 0:wd], ps_s[:, 2 * p:2 * p + 2, 0:wd],
                                         ACT.Exp, scale=LOGIT_SCALE).then_inc(s_p, 1)

            def copy_out(b, n):
                act.wait_ge(s_pv, NSTEP * b + GROUP_END[n] + 1)
                act.wait_ge(s_ot, NGRP * b + max(n - 1, 0))
                nc.scalar.copy(out_t[:, n % 2], ps_o[:]).then_inc(s_oc, 1)

            def batch(b, more):
                for k in range(NSTEP):
                    if k == 0 or STEPS[k - 1][0] != STEPS[k][0]:
                        exponents(b, k)
                    if k + 1 < NSTEP and STEPS[k + 1][0] == STEPS[k][0] and not (k in GROUP_END):
                        exponents(b, k + 1)
                    if k in GROUP_END:
                        copy_out(b, GROUP_END.index(k))
                        if k + 1 < NSTEP and STEPS[k + 1][0] == STEPS[k][0]:
                            exponents(b, k + 1)
                    if more:
                        keep_positive(b + 1, k)

            for c in range(NCHUNK):
                keep_positive(0, c)
            first = batch
            with act.Fori(0, B - 1) as b:
                first(b, True)
            batch(B - 1, False)

        @block.gpsimd
        def _(pool):
            link, restart, step = chain_on(pool, s_chp)
            link(nc.gpsimd.memset(v_op[:, :, :, DK:VW], 0.0))
            link(nc.gpsimd.memset(k_op[64:KC], 1.0))
            nc.gpsimd.memset(v_op[:, :, :, DK:DK + 1], 1.0).then_inc(s_init, 1)
            pool.wait_ge(s_init, 1)

            def combine(n):
                restart()
                link(nc.gpsimd.tensor_copy(iw_cur[:], iw_all[:, bass.ds(TILES * n, TILES), :]))
                for c, (i, c0, wd, h) in enumerate(CHUNKS):
                    dst = index[:, i % 2, c0:c0 + wd]
                    weight = iw_cur[:, i, h:h + 1]
                    if h == 0 and c0 == 0 and (i >= 2 or not isinstance(n, int)):
                        pool.wait_ge(s_sel, TILES * n + i - 1)
                    pool.wait_ge(s_relu, NCHUNK * n + c + 1)
                    step()
                    r = relu[:, c % 4, 0:wd]
                    if h == 0:
                        last = nc.gpsimd.tensor_scalar(dst, r, weight, 0.0, ALU.mult, ALU.add)
                    else:
                        link(nc.gpsimd.tensor_scalar(r, r, weight, 0.0, ALU.mult, ALU.add))
                        pool.wait_ge(s_relu_used, NCHUNK * n + c)
                        last = nc.gpsimd.tensor_tensor(dst, dst, r, ALU.add)
                    last.then_inc(s_relu_used, 1)
                    if h == IH - 1 and c0 + wd == P * (i + 1):
                        diag = index[:, i % 2, P * i:P * (i + 1)]
                        pool.wait_ge(s_relu_used, NCHUNK * n + c + 1)
                        step()
                        nc.gpsimd.affine_select(out=diag, in_=diag, compare_op=ALU.is_ge, fill=NOT_CAUSAL, base=0,
                                                pattern=[[-1, P]], channel_multiplier=1).then_inc(s_index, 1)

            def place_values(b):
                pool.wait_ge(s_pv, NSTEP * b)
                pool.wait_ge(s_init, 1)
                nc.gpsimd.tensor_copy(v_op[:, :, :, 0:DK],
                                      v_all[:, bass.ds(TILES * b, TILES), :].rearrange("p j (h d) -> p j h d", h=HEADS)
                                      ).then_inc(s_v, 1)

            def store(b):
                pool.wait_ge(s_norm, NGRP * b + NGRP)
                pool.dma_start(t["rows"][b], rows_out[:]).then_inc(s_st, 16)

            combine(0)
            with pool.Fori(0, B - 1) as b:
                place_values(b)
                combine(b + 1)
                store(b)
            place_values(B - 1)
            store(B - 1)

        @block.vector
        def _(dve):
            link, restart, _ = chain_on(dve, s_chv)

            def select(n, i):
                wd = P * (i + 1)
                dve.wait_ge(s_index, TILES * n + i + 1)
                link(nc.vector.memset(best[:], 0.0))
                cur = index[:, i % 2, 0:wd]
                for _ in range(TOPK // 8):
                    link(nc.vector.max(best[:], cur))
                    link(nc.vector.match_replace(cur, best[:], cur, TAKEN))
                nc.vector.tensor_scalar(hidden[:, i, 0:wd], cur, TAKEN, HIDE, ALU.is_gt,
                                        ALU.mult).then_inc(s_sel, 1)

            def take_turned(b):
                for j in range(TILES):
                    dve.wait_ge(s_turned, TILES * b + j + 1)
                    wd = S - P * j
                    if j == 0 and not (isinstance(b, int) and b == 0):
                        dve.wait_ge(s_sc, NPAIR * b)
                    nc.vector.tensor_copy(hidden_t[:, j, P * j:S], turn_banks[j % 2][:, 0:wd]).then_inc(s_hid, 1)

            def maxima(b, hg):
                for m in range(NMAX):
                    i = m // HL
                    dve.wait_ge(s_ms, NMAX * (HG * b + hg) + m + 1)
                    if P * (i + 1) <= BANK:
                        src, axis = ps_s[:, 2 * (m % 2), 0:P * (i + 1)], AX.X
                    else:
                        src = ps_s[:].rearrange("p c t -> p (c t)")[:, 2 * BANK * (m % 2):2 * BANK * (m % 2) + P * (i + 1)]
                        axis = AX.X
                    last = nc.vector.tensor_reduce(top[:, TILES * (m % HL) + i:TILES * (m % HL) + i + 1], src, axis, ALU.max)
                    last.then_inc(s_mt, 1)
                dve.wait_ge(s_mt, NMAX * (HG * b + hg + 1))
                link(nc.vector.memset(best[:], 0.0))
                nc.vector.memset(best[:], 0.0).then_inc(s_mtop, 1)
                dve.wait_ge(s_mturn, HG * b + hg + 1)
                if not (isinstance(b, int) and b == 0 and hg == 0):
                    dve.wait_ge(s_cl, 16 * PARTS * (HG * b + hg))
                link(nc.vector.tensor_scalar(neg[:, 0], ps_t[0:NMAX, 0:P], -1.0, None, ALU.mult))
                link(nc.vector.tensor_copy(neg_parts[:, 0], neg[:, 0]))
                link(nc.vector.tensor_tensor(neg[:, 1], neg[:, 0], neg_parts[:, 0], ALU.subtract))
                link(nc.vector.tensor_copy(neg_parts[:, 1], neg[:, 1]))
                nc.vector.tensor_tensor(neg_parts[:, 2], neg[:, 1], neg_parts[:, 1],
                                        ALU.subtract).then_inc(s_neg, 1)

            def normalise(b, n):
                hg, g = n // GROUPS, n % GROUPS
                dve.wait_ge(s_ot, NGRP * b + n + 1)
                if n == 0 and not (isinstance(b, int) and b == 0):
                    dve.wait_ge(s_st, 16 * b)
                src = ps_t[:].rearrange("p (c h v) -> p c h v", c=4, h=HL)
                link(nc.vector.reciprocal(recip[:], src[:, :, :, DK]))
                dst = rows_out[:, 4 * g:4 * g + 4, 32 * hg:32 * hg + 32].rearrange("p c (h d) -> p c h d", h=HL)
                rb = recip[:].rearrange("p c (h o) -> p c h o", o=1).broadcast_to([P, 4, HL, DK])
                nc.vector.tensor_tensor(dst, src[:, :, :, 0:DK], rb, ALU.mult).then_inc(s_norm, 1)

            def batch(b, more):
                restart()
                take_turned(b)
                dve.wait_ge(s_hid, TILES * b + TILES)
                for hg in range(HG):
                    maxima(b, hg)
                    for what, n in VECTOR_ORDER[hg]:
                        if what == "norm":
                            normalise(b, n)
                        elif more:
                            select(b + 1, n)

            for i in range(TILES):
                select(0, i)
            with dve.Fori(0, B - 1) as b:
                batch(b, True)
            batch(B - 1, False)


def finish_all(nc, t):
    with ExitStack() as ctx:
        def sb(name, shape, dt):
            return ctx.enter_context(nc.sbuf_tensor(name, shape, dt))

        def sem(name):
            return ctx.enter_context(nc.semaphore(name))

        NT = BANK // P
        NH = STATE // P
        ident = sb("identF", [P, P], F32)
        wo = sb("wo", [P, D], F32)
        w1 = sb("w1", [P, STATE], F32)
        w2 = sb("w2", [P, NH, D], F32)
        b1 = sb("b1", [P, NH], F32)
        b2 = sb("b2", [P, D], F32)
        xs = sb("xf", [P, 2, NT, D], F32)
        orow = sb("orow", [P, 2, NT, D], F32)
        oT = sb("oTf", [P, BANK], F32)
        x2 = sb("x2", [P, 2, NT, D], F32)
        stats = sb("statsf", [P, NT, 6], F32)
        mv = sb("mvf", [P, NT, 2], F32)
        std = sb("stdf", [P, NT], F32)
        rstd = sb("rstdf", [P, NT], F32)
        xn = sb("xnf", [P, NT, D], F32)
        xT = sb("xTf", [P, BANK], F32)
        h = sb("h", [P, NH, BANK], F32)
        res = sb("res", [P, 2, NT, D], F32)
        ps = ctx.enter_context(nc.psum_tensor("psf", [P, 8, BANK], F32))

        s_w = sem("ffn_weights_loaded")
        s_x = [sem(f"rows_loaded{e}") for e in range(2)]
        s_ot = sem("attn_turned")
        s_oT = sem("attn_t_copied")
        s_pr = sem("attn_projected")
        s_x2 = sem("x2_ready")
        s_bn = sem("moments2_ready")
        s_std = sem("std2_ready")
        s_xn = sem("xn2_ready")
        s_t = sem("xn2_turned")
        s_xT = sem("xn2_t_copied")
        s_h = sem("hidden_products")
        s_g = sem("gelu_done")
        s_y = sem("ffn_products")
        s_res = sem("result_ready")
        s_st = sem("result_stored")
        s_ch = sem("vector_chain_f")
        block = ctx.enter_context(nc.Block())

        @block.sync
        def _(sp):
            for dst, name in ((ident, "ident"), (wo, "wo"), (w1, "w1"), (w2, "w2"), (b1, "b1"), (b2, "b2")):
                sp.dma_start(dst[:], t[name]).then_inc(s_w, 16)

            def load(b, half):
                sp.dma_start(xs[:, half], t["x"][b, half]).then_inc(s_x[half], 16)
                sp.dma_start(orow[:, half], t["rows"][b, :, NT * half:NT * (half + 1)]).then_inc(s_x[half], 16)

            load(0, 0)
            load(0, 1)

            def batch(b, more):
                for half in range(2):
                    n = 2 * b + half
                    if more:
                        sp.wait_ge(s_x2, n + 1)
                        load(b + 1, half)
                    sp.wait_ge(s_res, n + 1)
                    sp.dma_start(t["out"][b, half], res[:, half]).then_inc(s_st, 16)

            with sp.Fori(0, B - 1) as b:
                batch(b, True)
            batch(B - 1, False)
            sp.wait_ge(s_st, 16 * 2 * B)

        @block.tensor
        def _(pe):
            pe.wait_ge(s_w, 96)
            with pe.Fori(0, B) as b:
                for half in range(2):
                    n = 2 * b + half
                    pe.wait_ge(s_x[half], 32 * b + 32)
                    for j in range(NT):
                        last = nc.tensor.transpose(ps[:, 0, P * j:P * (j + 1)], orow[:, half, j], ident[:])
                    last.then_inc(s_ot, 1)
                    pe.wait_ge(s_x2, n)
                    pe.wait_ge(s_oT, n + 1)
                    for j in range(NT):
                        last = nc.tensor.matmul(ps[:, 1, P * j:P * (j + 1)], oT[:, P * j:P * (j + 1)], wo[:],
                                                start=True, stop=True)
                    last.then_inc(s_pr, 1)
                    pe.wait_ge(s_xT, n)
                    pe.wait_ge(s_xn, n + 1)
                    for j in range(NT):
                        last = nc.tensor.transpose(ps[:, 2, P * j:P * (j + 1)], xn[:, j], ident[:])
                    last.then_inc(s_t, 1)
                    pe.wait_ge(s_g, NH * n)
                    pe.wait_ge(s_xT, n + 1)
                    for m in range(NH):
                        nc.tensor.matmul(ps[:, 3 + m], w1[:, P * m:P * (m + 1)], xT[:], start=True,
                                         stop=True).then_inc(s_h, 1)
                    pe.wait_ge(s_res, n)
                    pe.wait_ge(s_g, NH * n + NH)
                    for j in range(NT):
                        for m in range(NH):
                            last = nc.tensor.matmul(ps[:, 7, P * j:P * (j + 1)], h[:, m, P * j:P * (j + 1)],
                                                    w2[:, m], start=(m == 0), stop=(m == NH - 1))
                    last.then_inc(s_y, 1)

        @block.scalar
        def _(act):
            act.wait_ge(s_w, 96)
            with act.Fori(0, B) as b:
                for half in range(2):
                    n = 2 * b + half
                    act.wait_ge(s_pr, n)
                    act.wait_ge(s_ot, n + 1)
                    nc.scalar.copy(oT[:], ps[:, 0]).then_inc(s_oT, 1)
                    act.wait_ge(s_bn, n + 1)
                    nc.scalar.activation(std[:], mv[:, :, 1], ACT.Sqrt, bias=EPS).then_inc(s_std, 1)
                    act.wait_ge(s_h, NH * n)
                    act.wait_ge(s_t, n + 1)
                    nc.scalar.copy(xT[:], ps[:, 2]).then_inc(s_xT, 1)
                    for m in range(NH):
                        act.wait_ge(s_y, n)
                        act.wait_ge(s_h, NH * n + m + 1)
                        nc.scalar.activation(h[:, m], ps[:, 3 + m], ACT.Gelu, bias=b1[:, m:m + 1]).then_inc(s_g, 1)

        @block.vector
        def _(dve):
            link, restart, _ = chain_on(dve, s_ch)
            dve.wait_ge(s_w, 96)
            with dve.Fori(0, B) as b:
                restart()
                for half in range(2):
                    n = 2 * b + half
                    dve.wait_ge(s_x[half], 32 * b + 32)
                    dve.wait_ge(s_pr, n + 1)
                    cur = x2[:, half].rearrange("p j d -> p (j d)")
                    nc.vector.tensor_tensor(cur, ps[:, 1], xs[:, half].rearrange("p j d -> p (j d)"),
                                            ALU.add).then_inc(s_x2, 1)
                    dve.wait_ge(s_x2, n + 1)
                    for j in range(NT):
                        link(nc.vector.bn_stats(stats[:, j], x2[:, half, j]))
                    for j in range(NT):
                        last = nc.vector.bn_aggr(mv[:, j], stats[:, j])
                        if j < NT - 1:
                            link(last)
                    last.then_inc(s_bn, 1)
                    dve.wait_ge(s_std, n + 1)
                    link(nc.vector.reciprocal(rstd[:], std[:]))
                    dve.wait_ge(s_t, n)
                    for j in range(NT):
                        last = nc.vector.tensor_scalar(xn[:, j], x2[:, half, j], mv[:, j, 0:1], rstd[:, j:j + 1],
                                                       ALU.subtract, ALU.mult)
                    last.then_inc(s_xn, 1)
                    dve.wait_ge(s_xn, n + 1)
                    b2v = b2[:].rearrange("p (o d) -> p o d", o=1).broadcast_to([P, NT, D])
                    link(nc.vector.tensor_tensor(x2[:, half], x2[:, half], b2v, ALU.add))
                    dve.wait_ge(s_y, n + 1)
                    dve.wait_ge(s_st, 16 * b * 2)
                    nc.vector.tensor_tensor(res[:, half].rearrange("p j d -> p (j d)"), ps[:, 7], cur,
                                            ALU.add).then_inc(s_res, 1)


def build(nc, t):
    with ExitStack() as ctx:
        v_all = ctx.enter_context(nc.sbuf_tensor("v_all", [P, B * TILES, P], F32))
        iw_all = ctx.enter_context(nc.sbuf_tensor("iw_all", [P, B * TILES, IH], F32))
        project_all(nc, t, v_all, iw_all)
        attend_all(nc, t, v_all, iw_all)
        finish_all(nc, t)


def kernel(**inputs):
    import numpy as np
    import concourse.bacc as bacc
    from concourse.bass_utils import run_bass_kernel_spmd

    order = np.array([(hg * HL + hl) * DK + d for hg in range(HG) for d in range(DK) for hl in range(HL)])
    swap = order ^ 1
    qkv = np.asarray(inputs["L0_attn_qkv_w"])
    wq, wk, wv = qkv[0:D], qkv[D:2 * D], qkv[2 * D:3 * D]
    w = np.concatenate([wq[order], wq[swap], wk[order], wk[swap], np.asarray(inputs["L0_attn_iq_w"]),
                        np.asarray(inputs["L0_attn_ik_w"]), wv, np.asarray(inputs["L0_attn_iw_w"])], axis=0)
    w = np.ascontiguousarray(w.T)
    f32 = np.float32
    inv = (f32(1.0) / np.power(f32(1250.0), np.arange(0, DK, 2, dtype=f32) / f32(DK))).astype(f32)
    freqs = np.outer(np.arange(S, dtype=f32), inv).astype(f32)
    ch = order % DK
    cos = np.ascontiguousarray(np.cos(freqs)[:, ch // 2].T.astype(f32))
    sin = np.ascontiguousarray((np.sin(freqs)[:, ch // 2] * np.where(ch % 2 == 0, -1.0, 1.0)).T.astype(f32))
    eye = np.eye(P, dtype=f32)
    import ml_dtypes
    given = {
        "x": np.asarray(inputs["L0_attn_x"]),
        "w": w, "cos": cos, "sin": sin, "ident": eye, "identb": eye.astype(ml_dtypes.bfloat16),
        "wo": np.ascontiguousarray(np.asarray(inputs["L0_attn_wo_w"]).T),
        "w1": np.asarray(inputs["L0_ffn_w1"]), "w2": np.asarray(inputs["L0_ffn_w2"]),
        "b1": np.asarray(inputs["L0_ffn_b1"]).reshape(STATE // P, P).T, "b2": np.asarray(inputs["L0_ffn_b2"]),
    }
    nc = bacc.Bacc("TRN2", target_bir_lowering=False, num_devices=1)
    t = {}
    arrays = {}
    for name, a in given.items():
        a = np.ascontiguousarray(a)
        arrays["in_" + name] = a
        t[name] = nc.dram_tensor("in_" + name, a.shape, mybir.dt.from_np(a.dtype), kind="ExternalInput").ap()
    NT = BANK // P
    t["x"] = t["x"].rearrange("b (g j p) d -> b g p j d", g=2, p=P)
    t["w2"] = t["w2"].rearrange("(m p) d -> p m d", p=P)
    t["b2"] = t["b2"].rearrange("(o d) -> o d", o=1).broadcast_to([P, D])
    for name in ("q", "k", "iq0", "iq1", "ik"):
        rows = ID if name == "ik" else P
        t[name + "_parts"] = nc.dram_tensor(name + "_parts", (B, PARTS, rows, S), BF16, kind="Internal").ap()
    t["rows"] = nc.dram_tensor("attn_rows", (B, P, TILES, D), F32, kind="Internal").ap()
    out = nc.dram_tensor("out_0", (B, S, D), F32, kind="ExternalOutput").ap()
    t["out"] = out.rearrange("b (g j p) d -> b g p j d", g=2, p=P)
    build(nc, t)
    r = run_bass_kernel_spmd(nc, [arrays], core_ids=[0])
    return r.results[0]["out_0"]
```

```python
from contextlib import ExitStack

import concourse.bass as bass
from concourse import mybir

F32 = mybir.dt.float32
BF16 = mybir.dt.bfloat16
ALU = mybir.AluOpType
ACT = mybir.ActivationFunctionType
AX = mybir.AxisListType

P = 128
BANK = 512
B, S, D = 4, 1024, 128
HEADS, DK = 16, 8
IH, ID = 4, 64
TOPK = 64
STATE = 512
HG, HL = 4, 4
TILES = S // P
GROUPS = S // BANK
PARTS = 3
KROWS = PARTS * PARTS * DK
KC = KROWS + PARTS
VW = 32
EPS = 1e-5
NOT_CAUSAL = -1.0e9
TAKEN = -3.0e38
HIDE = -1.0e30
SAFE = 40.0
LOGIT_SCALE = float(DK) ** -0.5

STEPS = [(hg, g, j) for hg in range(HG) for g in range(GROUPS) for j in range(4 * g + 4)]
CHUNKS = [(i, c, min(BANK, P * (i + 1) - c), h)
          for i in range(TILES) for c in range(0, P * (i + 1), BANK) for h in range(IH)]
NSTEP, NCHUNK, NPAIR = len(STEPS), len(CHUNKS), 2 * len(STEPS)
assert NSTEP == NCHUNK == 48
NGRP = HG * GROUPS
HALF_CHUNKS = 16
GROUP_END = [k for k in range(NSTEP) if k + 1 == NSTEP or STEPS[k + 1][:2] != STEPS[k][:2]]
ROUNDS = TOPK // 8


def plan_batch():
    wide = [max(P, BANK * (g + 1) - max(P * j, BANK * g)) for _, g, j in STEPS]
    done = [sum(wide[:k + 1]) / sum(wide) for k in range(NSTEP)]
    cost = [2.2 + i for i in range(TILES)]
    start = [sum(cost[:i]) / sum(cost) for i in range(TILES + 1)]
    chunks_at = [[] for _ in range(NSTEP)]
    for c, (i, _, _, _) in enumerate(CHUNKS):
        mine = [x for x, ch in enumerate(CHUNKS) if ch[0] == i]
        aim = 0.0 if i == 0 else start[i - 1] + (start[i] - start[i - 1]) * 0.9 * (c - mine[0]) / len(mine)
        if i:
            chunks_at[next(k for k in range(NSTEP) if done[k] >= aim)].append(c)
    events = {}
    todo = [(done[k + 1] if k + 1 < NSTEP else 2.0, "norm", n) for n, k in enumerate(GROUP_END)]
    todo += [(done[(NSTEP // HG) * hg - 2] if hg else -1.0, "max", hg) for hg in range(HG)]
    for when, what, n in sorted(todo):
        i = max([x for x in range(TILES) if start[x] <= when], default=0)
        at = (i, min(ROUNDS, int(ROUNDS * max(when - start[i], 0) / (start[i + 1] - start[i]))))
        events.setdefault(at, []).append((what, n))
    return chunks_at, events


CHUNKS_AT, EVENTS = plan_batch()
EARLY = IH
QK_DMAS = 3 + 5
INDEX_DMAS = 6 + 4


def span(k):
    _, g, j = STEPS[k]
    t0 = max(P * j, BANK * g)
    return t0, BANK * (g + 1) - t0


def chain_on(eng, sem):
    count = [0]

    def link(ins):
        count[0] += 1
        ins.then_inc(sem, 1)
        eng.wait_ge(sem, count[0])

    def restart():
        count[0] = 0
        eng.sem_clear(sem)

    def step():
        count[0] += 1
        eng.sem_inc(sem, 1)
        eng.wait_ge(sem, count[0])

    return link, restart, step


def project_all(nc, t, v_all, iw_all, peak):
    with ExitStack() as ctx:
        def sb(name, shape, dt):
            return ctx.enter_context(nc.sbuf_tensor(name, shape, dt))

        def sem(name):
            return ctx.enter_context(nc.semaphore(name))

        NT = BANK // P
        NW = 7 * P + IH
        COL = dict(q=0, qs=P, k=2 * P, ks=3 * P, iq0=4 * P, iq1=5 * P, ik=6 * P, v=6 * P + ID)
        w = sb("w", [P, NW + ID], F32)
        cos = sb("cos", [P, S], F32)
        sin = sb("sin", [P, S], F32)
        ident = sb("identA", [P, P], F32)
        power = sb("power", [P, NT], F32)
        head_of = sb("head_of", [P, HEADS], BF16)
        squares = sb("squares", [P, 2, BANK], BF16)
        xs = sb("xs", [P, 2, NT, D], F32)
        stats = sb("stats", [P, NT, 6], F32)
        mv = sb("mv", [P, NT, 2], F32)
        var = sb("var", [P, NT], F32)
        rstd = sb("rstd", [P, NT], F32)
        xn = sb("xn", [P, NT, D], F32)
        xT = sb("xT", [P, 2, BANK], F32)
        by_cos = sb("by_cos", [P, 2, BANK], F32)
        by_sin = sb("by_sin", [P, 2, BANK], F32)
        rot = sb("rot", [P, 2, BANK], F32)
        rest = sb("rest", [P, 5, BANK], F32)
        parts = sb("parts", [P, 5, PARTS, BANK], BF16)
        ps = ctx.enter_context(nc.psum_tensor("psx", [P, 8, BANK], F32))

        s_w = sem("weights_loaded")
        s_x = [sem(f"x_loaded{h}") for h in range(2)]
        s_pow = sem("power_filled")
        s_var = sem("variances_ready")
        s_rstd = sem("rstd_ready")
        s_xn = sem("xn_ready")
        s_t = sem("xn_turned")
        s_xT = sem("xT_copied")
        s_mm = sem("projected")
        s_rc = sem("rope_products")
        s_rot = sem("rotated")
        s_sq = sem("squares_ready")
        s_nm = sem("norms_ready")
        s_peak = sem("peaks_taken")
        s_hi = sem("high_parts")
        s_r = sem("rests_ready")
        s_mid = sem("middle_parts")
        s_lo = sem("low_parts")
        s_st = sem("operands_stored")
        s_v = sem("values_copied")
        s_ch = sem("vector_chain_a")
        block = ctx.enter_context(nc.Block())

        PROD = [("q", 1), ("qs", 2), ("k", 3), ("ks", 4), ("iq0", 5), ("iq1", 6), ("ik", 7)]
        SPLIT = ["q", "k", "iq0", "iq1", "ik"]
        NPROD, NSPLIT = len(PROD) + 2, len(SPLIT)

        def rows_of(name):
            return ID if name == "ik" else P

        def whole(a):
            return rot[:, a] if a < 2 else ps[0:rows_of(SPLIT[a]), 3 + a]

        @block.sync
        def _(sp):
            def load(b, half):
                sp.dma_start(xs[:, half], t["x"][b, half]).then_inc(s_x[half], 16)

            load(0, 0)
            sp.dma_start(ident[:], t["ident"]).then_inc(s_w, 16)
            sp.dma_start(w[:], t["w"]).then_inc(s_w, 16)
            sp.dma_start(cos[:], t["cos"]).then_inc(s_w, 16)
            sp.dma_start(sin[:], t["sin"]).then_inc(s_w, 16)
            sp.dma_start(head_of[:], t["head_of"]).then_inc(s_w, 16)
            load(0, 1)

            def batch(b, more):
                for half in range(2):
                    n = 2 * b + half
                    if more:
                        sp.wait_ge(s_xn, n + 1)
                        load(b + 1, half)
                    for a, name in enumerate(SPLIT):
                        sp.wait_ge(s_mid, NSPLIT * n + a + 1)
                        sp.wait_ge(s_lo, NSPLIT * n + a + 1)
                        cols = slice(half * BANK, (half + 1) * BANK)
                        sp.dma_start(t[name + "_parts"][b, :, :, cols].rearrange("p c t -> c p t"),
                                     parts[0:rows_of(name), a]).then_inc(s_st, 16)

            with sp.Fori(0, B - 1) as b:
                batch(b, True)
            batch(B - 1, False)
            sp.wait_ge(s_st, 16 * NSPLIT * 2 * B)

        @block.vector
        def _(dve):
            link, restart, _ = chain_on(dve, s_ch)

            def normalise(b, half):
                n = 2 * b + half
                x = xs[:, half]
                dve.wait_ge(s_x[half], 16 * b + 16)
                for j in range(NT):
                    link(nc.vector.bn_stats(stats[:, j], x[:, j]))
                for j in range(NT):
                    link(nc.vector.bn_aggr(mv[:, j], stats[:, j]))
                nc.vector.tensor_scalar(var[:], mv[:, :, 1], EPS, None, ALU.add).then_inc(s_var, 1)
                dve.wait_ge(s_rstd, n + 1)
                dve.wait_ge(s_t, n)
                for j in range(NT):
                    last = nc.vector.tensor_scalar(xn[:, j], x[:, j], mv[:, j, 0:1], rstd[:, j:j + 1],
                                                   ALU.subtract, ALU.mult)
                last.then_inc(s_xn, 1)

            def rest_of(n, a):
                rows = rows_of(SPLIT[a])
                dve.wait_ge(s_lo, NSPLIT * n)
                dve.wait_ge(s_hi, NSPLIT * n + a + 1)
                nc.vector.tensor_tensor(rest[0:rows, a], whole(a), parts[0:rows, a, 0],
                                        ALU.subtract).then_inc(s_r, 1)

            def batch(b, more):
                restart()
                for half in range(2):
                    n = 2 * b + half
                    cols = slice(half * BANK, (half + 1) * BANK)
                    for a in range(2):
                        dve.wait_ge(s_mm, NPROD * n + 2 * a + 2)
                        dve.wait_ge(s_rot, 2 * n + a)
                        nc.vector.tensor_tensor(by_cos[:, a], ps[:, 1 + 2 * a], cos[:, cols], ALU.mult)
                        nc.vector.tensor_tensor(by_sin[:, a], ps[:, 2 + 2 * a], sin[:, cols],
                                                ALU.mult).then_inc(s_rc, 1)
                    if half == 0:
                        normalise(b, 1)
                    elif more:
                        normalise(b + 1, 0)
                    for a in range(NSPLIT):
                        rest_of(n, a)
                    for a in range(2):
                        dve.wait_ge(s_nm, 2 * n + a + 1)
                        nc.vector.tensor_reduce(peak[:, a, bass.ds(n, 1)], ps[0:HEADS, 3 + a], AX.X,
                                                ALU.max).then_inc(s_peak, 1)

            dve.wait_ge(s_w, 80)
            normalise(0, 0)
            with dve.Fori(0, B - 1) as b:
                batch(b, True)
            batch(B - 1, False)

        @block.scalar
        def _(act):
            def turned(n, half):
                act.wait_ge(s_mm, NPROD * (n - 1)) if not isinstance(n, int) or n >= 1 else None
                act.wait_ge(s_t, n + 1)
                nc.scalar.copy(xT[:, half], ps[:, 0]).then_inc(s_xT, 1)

            def high(n, a):
                rows = rows_of(SPLIT[a])
                act.wait_ge(s_st, 16 * NSPLIT * n)
                if a < 2:
                    act.wait_ge(s_rot, 2 * n + a + 1)
                else:
                    act.wait_ge(s_mm, NPROD * n + 3 + a)
                nc.scalar.copy(parts[0:rows, a, 0], whole(a)).then_inc(s_hi, 1)

            def middle(n, a):
                rows = rows_of(SPLIT[a])
                act.wait_ge(s_r, NSPLIT * n + a + 1)
                nc.scalar.copy(parts[0:rows, a, 1], rest[0:rows, a]).then_inc(s_mid, 1)

            def values(n):
                for e in range(2):
                    act.wait_ge(s_mm, NPROD * n + 8 + e)
                    src = ps[:, 1 + e, 0:2 * (P + IH)].rearrange("p (j c) -> p j c", j=2)
                    tile = NT * n + 2 * e
                    nc.scalar.copy(v_all[:, bass.ds(tile, 2), :], src[:, :, 0:P])
                    nc.scalar.copy(iw_all[:, bass.ds(tile, 2), :], src[:, :, P:P + IH]).then_inc(s_v, 1)

            def batch(b, more):
                for half in range(2):
                    n = 2 * b + half
                    high(n, 0)
                    high(n, 1)
                    for a in range(2):
                        act.wait_ge(s_nm, 2 * n)
                        nc.scalar.activation(squares[:, a], rot[:, a], ACT.Square).then_inc(s_sq, 1)
                    for a in range(2, NSPLIT):
                        high(n, a)
                    middle(n, 0)
                    middle(n, 1)
                    values(n)
                    if half == 0 or more:
                        turned(n + 1, 1 - half)
                    for a in range(2, NSPLIT):
                        middle(n, a)

            act.wait_ge(s_w, 80)
            turned(0, 0)
            with act.Fori(0, B - 1) as b:
                batch(b, True)
            batch(B - 1, False)

        @block.gpsimd
        def _(pool):
            def rstd_of(n):
                pool.wait_ge(s_var, n + 1)
                pool.wait_ge(s_xn, n)
                nc.gpsimd.tensor_tensor(rstd[:], var[:], power[:], ALU.pow).then_inc(s_rstd, 1)

            def low(n, a):
                rows = rows_of(SPLIT[a])
                pool.wait_ge(s_mid, NSPLIT * n + a + 1)
                nc.gpsimd.tensor_tensor(parts[0:rows, a, 2], rest[0:rows, a], parts[0:rows, a, 1],
                                        ALU.subtract).then_inc(s_lo, 1)

            def batch(b, more):
                for half in range(2):
                    n = 2 * b + half
                    for a in range(2):
                        pool.wait_ge(s_r, NSPLIT * n)
                        pool.wait_ge(s_sq, 2 * n)
                        pool.wait_ge(s_rc, 2 * n + a + 1)
                        nc.gpsimd.tensor_tensor(rot[:, a], by_cos[:, a], by_sin[:, a], ALU.add).then_inc(s_rot, 1)
                    if half == 0 or more:
                        rstd_of(n + 1)
                    for a in range(NSPLIT):
                        low(n, a)

            nc.gpsimd.memset(power[:], -0.5).then_inc(s_pow, 1)
            pool.wait_ge(s_pow, 1)
            rstd_of(0)
            with pool.Fori(0, B - 1) as b:
                batch(b, True)
            batch(B - 1, False)

        @block.tensor
        def _(pe):
            def turn(n):
                if not isinstance(n, int) or n:
                    pe.wait_ge(s_xT, n)
                pe.wait_ge(s_xn, n + 1)
                for j in range(NT):
                    last = nc.tensor.transpose(ps[:, 0, P * j:P * (j + 1)], xn[:, j], ident[:])
                last.then_inc(s_t, 1)

            def batch(b, more):
                for half in range(2):
                    n = 2 * b + half
                    pe.wait_ge(s_xT, n + 1)
                    for a, (name, bank) in enumerate(PROD):
                        rows = rows_of(name)
                        if a < 2:
                            pe.wait_ge(s_v, 2 * n)
                        elif a < 4:
                            pe.wait_ge(s_peak, 2 * n)
                        else:
                            pe.wait_ge(s_r, NSPLIT * n)
                        nc.tensor.matmul(ps[0:rows, bank], w[:, COL[name]:COL[name] + rows], xT[:, half],
                                         start=True, stop=True).then_inc(s_mm, 1)
                    pe.wait_ge(s_rc, 2 * n + 1)
                    for e in range(2):
                        for j in range(2):
                            tile = 2 * e + j
                            last = nc.tensor.matmul(ps[:, 1 + e, (P + IH) * j:(P + IH) * (j + 1)],
                                                    xT[:, half, P * tile:P * (tile + 1)],
                                                    w[:, COL["v"]:COL["v"] + P + IH], start=True, stop=True)
                        last.then_inc(s_mm, 1)
                    pe.wait_ge(s_rc, 2 * n + 2)
                    for a in range(2):
                        pe.wait_ge(s_sq, 2 * n + a + 1)
                        nc.tensor.matmul(ps[0:HEADS, 3 + a], head_of[:], squares[:, a], start=True,
                                         stop=True).then_inc(s_nm, 1)
                    if half == 0 or more:
                        turn(n + 1)

            pe.wait_ge(s_w, 80)
            turn(0)
            with pe.Fori(0, B - 1) as b:
                batch(b, True)
            batch(B - 1, False)


def attend_all(nc, t, v_all, iw_all, peak):
    with ExitStack() as ctx:
        def sb(name, shape, dt):
            return ctx.enter_context(nc.sbuf_tensor(name, shape, dt))

        def sem(name):
            return ctx.enter_context(nc.semaphore(name))

        ident = sb("ident", [P, P], F32)
        identb = sb("identb", [P, P], BF16)
        q_op = sb("q_op", [KC, 2, HL, S], BF16)
        k_op = sb("k_op", [KC, 2, HL, S], BF16)
        v_op = sb("v_op", [P, TILES, HEADS, VW], F32)
        iq_op = sb("iq_op", [P, 2, 3, IH, BANK], BF16)
        ik_op = sb("ik_op", [P, 2, 2, S], BF16)
        iw_cur = sb("iw_cur", [P, TILES, IH], F32)
        hidden = sb("hidden", [P, TILES, S], BF16)
        hidden_t = sb("hidden_t", [P, TILES, S], BF16)
        probs = sb("probs", [P, 2, HL, BANK], F32)
        relu = sb("relu", [P, 4, BANK], F32)
        index = sb("index", [P, 2, S], F32)
        best = sb("best", [P, 8], F32)
        out_t = sb("out_t", [P, 2, BANK], F32)
        recip = sb("recip", [P, 4, HL], F32)
        rows_out = sb("rows_out", [P, TILES, D], F32)
        top = sb("top", [P, TILES * HL], F32)
        peaks = sb("peaks", [HEADS, 2], F32)
        peak_product = sb("peak_product", [HEADS, 1], F32)
        bound = sb("bound", [1, 4], F32)
        exact_flag = sb("exact_flag", [1, 1], mybir.dt.int32)
        shift_row = sb("shift_row", [1, BANK], BF16)
        neg = sb("neg", [TILES * HL, 3, P], F32)
        neg_parts = sb("neg_parts", [TILES * HL, PARTS, P], BF16)

        ps_s = ctx.enter_context(nc.psum_tensor("ps_s", [P, 4, BANK], F32))
        ps_o = ctx.enter_context(nc.psum_tensor("ps_o", [P, BANK], F32))
        ps_d = ctx.enter_context(nc.psum_tensor("ps_d", [P, 2, BANK], F32))
        ps_t = ctx.enter_context(nc.psum_tensor("ps_t", [P, BANK], F32))
        turn_banks = [ps_t[:].bitcast(BF16), ps_d[:, 0].bitcast(BF16),
                      ps_s[:, 2].bitcast(BF16), ps_s[:, 3].bitcast(BF16)]

        s_id = sem("identities_loaded")
        s_init = sem("operands_filled")
        s_qk = [sem(f"qk_loaded{r}") for r in range(2)]
        s_iqk = [sem(f"index_operands_loaded{r}") for r in range(2)]
        s_dots = sem("dots_ready")
        s_relu = sem("relu_ready")
        s_relu_used = sem("relu_used")
        s_index = sem("index_ready")
        s_sel = sem("selected")
        s_turned = sem("selection_turned")
        s_hid = [sem("hidden_t_even_ready"), sem("hidden_t_odd_ready")]
        s_v = sem("values_placed")
        s_sc = sem("logits_ready")
        s_p = sem("probs_ready")
        s_pv = sem("pv_done")
        s_oc = sem("out_copied")
        s_ot = sem("out_turned")
        s_norm = sem("normalised")
        s_ms = sem("max_logits_ready")
        s_mt = sem("max_taken")
        s_mtop = sem("maxima_ready")
        s_mturn = sem("maxima_turned")
        s_neg = sem("neg_parts_ready")
        s_cl = sem("max_rows_loaded")
        s_pk = sem("peak_product_ready")
        s_hb = sem("head_bounds_ready")
        s_bd = sem("bound_ready")
        s_sqb = sem("squared_bound_ready")
        s_root = sem("bound_root_ready")
        s_st = sem("rows_stored")
        s_chv = sem("vector_chain")
        s_chp = sem("pool_chain")
        s_chm = sem("maxima_chain")
        block = ctx.enter_context(nc.Block())

        NMAX = TILES * HL

        @block.sync
        def _(sp):
            sp.dma_start(ident[:], t["ident"]).then_inc(s_id, 16)
            sp.dma_start(identb[:], t["identb"]).then_inc(s_id, 16)

            def load_qk(b, hg):
                r = hg % 2
                rows = slice(32 * hg, 32 * hg + 32)
                q = t["q_parts"][b, :, rows, :].rearrange("p (d h) t -> p d (h t)", h=HL)
                k = t["k_parts"][b, :, rows, :].rearrange("p (d h) t -> p d (h t)", h=HL)
                G = PARTS * DK
                for rep in range(PARTS):
                    sp.dma_start(q_op[G * rep:G * rep + G, r].rearrange("p h t -> p (h t)"), q)\
                      .then_inc(s_qk[r], 16)
                    cut = DK * (PARTS - rep)
                    sp.dma_start(k_op[G * rep:G * rep + cut, r].rearrange("p h t -> p (h t)"), k[rep:])\
                      .then_inc(s_qk[r], 16)
                    if rep:
                        sp.dma_start(k_op[G * rep + cut:G * rep + G, r].rearrange("p h t -> p (h t)"), k[:rep])\
                          .then_inc(s_qk[r], 16)

            def load_index(b, half):
                n = BANK * (half + 1)
                for combo, pair in enumerate(((0, 0), (1, 1), (0, 2))):
                    for lo, part in enumerate(pair):
                        src = [t["iq0_parts"], t["iq1_parts"]]
                        for e in range(2):
                            sp.dma_start(
                                iq_op[ID * lo:ID * lo + ID, half, combo, 2 * e:2 * e + 2],
                                src[e][b, part, :, BANK * half:BANK * (half + 1)].rearrange("(h d) t -> d h t", h=2)
                            ).then_inc(s_iqk[half], 16)
                for combo, pair in enumerate(((0, 1), (2, 0))):
                    for lo, part in enumerate(pair):
                        sp.dma_start(ik_op[ID * lo:ID * lo + ID, half, combo, 0:n],
                                     t["ik_parts"][b, part, :, 0:n]).then_inc(s_iqk[half], 16)

            def load_maxima(b, hg):
                sp.wait_ge(s_neg, HG * b + hg + 1)
                sp.wait_ge(s_cl, 32)
                for p in range(PARTS):
                    dst = q_op[KROWS + p:KROWS + p + 1, hg % 2].rearrange("o h (i t) -> o (h i) t", i=TILES)
                    sp.dma_start(dst, neg_parts[:, p, :]).then_inc(s_cl, 16)

            load_index(0, 0)
            load_index(0, 1)
            sp.wait_ge(s_init, 1)
            load_qk(0, 0)
            load_qk(0, 1)
            sp.wait_ge(s_bd, 1)
            src = shift_row[:].rearrange("o (n t) -> o n t", n=1).broadcast_to([1, HL * S // BANK, BANK])
            for r in range(2):
                sp.dma_start(q_op[KROWS:KROWS + 1, r].rearrange("o h (n t) -> o (h n) t", t=BANK), src)\
                  .then_inc(s_cl, 16)
            exact = sp.value_load(exact_flag[0:1, 0:1], min_val=0, max_val=1)

            def next_index(b):
                sp.wait_ge(s_dots, NCHUNK * b)
                load_index(b, 0)
                load_index(b, 1)

            def batch(b, more, index):
                for hg in range(HG):
                    with sp.If(exact > 0):
                        load_maxima(b, hg)
                    if hg + 2 < HG or more:
                        sp.wait_ge(s_sc, NPAIR * b + (NPAIR // HG) * (hg + 1))
                        load_qk(b + (hg + 2) // HG, (hg + 2) % HG)
                    if hg == 2 and index:
                        next_index(b + 2)

            next_index(1)
            with sp.Fori(0, B - 2) as b:
                batch(b, True, True)
            batch(B - 2, True, False)
            batch(B - 1, False, False)
            sp.wait_ge(s_st, 16 * B)

        @block.tensor
        def _(pe):
            def dots(n, c):
                i, c0, wd, h = CHUNKS[c]
                half = i // 4
                if c == 0:
                    pe.wait_ge(s_iqk[0], 16 * 16 * n + 256)
                if c == HALF_CHUNKS:
                    pe.wait_ge(s_iqk[1], 16 * 16 * n + 256)
                if c >= 2 or not isinstance(n, int):
                    pe.wait_ge(s_relu, NCHUNK * n + c - 1)
                qc = slice(P * (i % 4), P * (i % 4) + P)
                for m, kc in enumerate((0, 0, 1)):
                    last = nc.tensor.matmul(ps_d[:, c % 2, 0:wd], iq_op[:, half, m, h, qc],
                                            ik_op[:, half, kc, c0:c0 + wd], start=(m == 0), stop=(m == 2))
                last.then_inc(s_dots, 1)

            def turn_selection(b, more):
                pe.wait_ge(s_relu, NCHUNK * b + NCHUNK + (EARLY if more else 0))
                pe.wait_ge(s_p, NPAIR * b)
                pe.wait_ge(s_norm, NGRP * b)
                pe.wait_ge(s_sel, TILES * b + TILES)
                for j in range(TILES):
                    if j >= 4:
                        pe.wait_ge(s_hid[j % 2], TILES // 2 * b + (j - 4) // 2 + 1)
                    for i in range(j, TILES):
                        last = nc.tensor.transpose(turn_banks[j % 4][:, P * (i - j):P * (i - j + 1)],
                                                   hidden[:, i, P * j:P * (j + 1)], identb[:])
                    last.then_inc(s_turned, 1)

            def row_maxima(b, hg):
                r = hg % 2
                pe.wait_ge(s_p, NPAIR * b + (NPAIR // HG) * hg)
                for m in range(NMAX):
                    i, hl = m // HL, m % HL
                    if m >= 2:
                        pe.wait_ge(s_mt, NMAX * (HG * b + hg) + m - 1)
                    for c0 in range(0, P * (i + 1), BANK):
                        wd = min(BANK, P * (i + 1) - c0)
                        bank = ps_s[:, 2 * (m % 2) + c0 // BANK, 0:wd]
                        nc.tensor.matmul(bank, q_op[0:KROWS, r, hl, P * i:P * (i + 1)],
                                         k_op[0:KROWS, r, hl, c0:c0 + wd], start=True, stop=False,
                                         skip_group_check=True)
                        for j in range(c0 // P, (c0 + wd) // P):
                            last = nc.tensor.matmul(bank[:, P * j - c0:P * j - c0 + P],
                                                    hidden_t[:, j, P * i:P * (i + 1)], identb[:],
                                                    start=False, stop=(P * (j + 1) == c0 + wd),
                                                    skip_group_check=True)
                    last.then_inc(s_ms, 1)
                pe.wait_ge(s_mtop, HG * b + hg + 1)
                nc.tensor.transpose(ps_s[0:NMAX, 0, 0:P], top[:], ident[:]).then_inc(s_mturn, 1)
                pe.wait_ge(s_cl, 32 + 16 * PARTS * (HG * b + hg + 1))

            def logits(b, k):
                hg, g, j = STEPS[k]
                r = hg % 2
                t0, wd = span(k)
                for p in range(2):
                    pe.wait_ge(s_p, NPAIR * b + max(2 * k + p - 1, 0))
                    for e in range(2):
                        nc.tensor.matmul(ps_s[:, 2 * p + e, 0:wd], identb[:], hidden_t[:, j, t0:t0 + wd],
                                         start=True, stop=False)
                    for e in range(2):
                        last = nc.tensor.matmul(ps_s[:, 2 * p + e, 0:wd], k_op[:, r, 2 * p + e, P * j:P * (j + 1)],
                                                q_op[:, r, 2 * p + e, t0:t0 + wd], start=False, stop=True)
                    last.then_inc(s_sc, 1)

            def weigh(b, k):
                hg, g, j = STEPS[k]
                t0, wd = span(k)
                n = GROUPS * hg + g
                if k == 0:
                    pe.wait_ge(s_v, b + 1)
                if j == 0 and not (isinstance(b, int) and b == 0 and n == 0):
                    pe.wait_ge(s_oc, NGRP * b + n)
                pe.wait_ge(s_p, NPAIR * b + 2 * k + 2)
                for hl in range(HL):
                    last = nc.tensor.matmul(ps_o[VW * hl:VW * (hl + 1), t0 - BANK * g:BANK],
                                            v_op[:, j, HL * hg + hl, :], probs[:, k % 2, hl, 0:wd],
                                            start=(j == 0), stop=(k in GROUP_END))
                last.then_inc(s_pv, 1)

            def turn_out(b, n):
                pe.wait_ge(s_oc, NGRP * b + n + 1)
                if n:
                    pe.wait_ge(s_norm, NGRP * b + n)
                for c in range(4):
                    last = nc.tensor.transpose(ps_t[:, P * c:P * (c + 1)], out_t[:, n % 2, P * c:P * (c + 1)],
                                               ident[:])
                last.then_inc(s_ot, 1)

            def begin(b, k):
                hg, g, j = STEPS[k]
                if g == 0 and j == 0:
                    pe.wait_ge(s_qk[hg % 2], 16 * QK_DMAS * (2 * b + hg // 2 + 1))
                    with pe.If(exact > 0):
                        row_maxima(b, hg)
                logits(b, k)

            def batch(b, more):
                if more:
                    for c in range(EARLY):
                        dots(b + 1, c)
                turn_selection(b, more)
                for half in range(2):
                    pe.wait_ge(s_hid[half], TILES // 2 * b + TILES // 2)
                begin(b, 0)
                for k in range(NSTEP):
                    if k + 1 < NSTEP:
                        begin(b, k + 1)
                    weigh(b, k)
                    if k - 1 in GROUP_END:
                        turn_out(b, GROUP_END.index(k - 1))
                    if more:
                        for c in CHUNKS_AT[k]:
                            dots(b + 1, c)
                turn_out(b, NGRP - 1)

            pe.wait_ge(s_id, 32)
            pe.wait_ge(s_pk, 1)
            nc.tensor.matmul(ps_t[0:1, 0:HEADS], peak_product[:], ident[0:HEADS, 0:HEADS], start=True, stop=True).then_inc(s_hb, 1)
            for c in range(NCHUNK):
                dots(0, c)
            pe.wait_ge(s_bd, 1)
            pe.wait_ge(s_cl, 32)
            exact = pe.value_load(exact_flag[0:1, 0:1], min_val=0, max_val=1)
            with pe.Fori(0, B - 1) as b:
                batch(b, True)
            batch(B - 1, False)

        @block.scalar
        def _(act):
            def keep_positive(n, c):
                i, c0, wd, h = CHUNKS[c]
                act.wait_ge(s_dots, NCHUNK * n + c + 1)
                if c >= 4 or not isinstance(n, int):
                    act.wait_ge(s_relu_used, NCHUNK * n + c - 3)
                nc.scalar.activation(relu[:, c % 4, 0:wd], ps_d[:, c % 2, 0:wd], ACT.Relu).then_inc(s_relu, 1)

            def exponents(b, k):
                t0, wd = span(k)
                act.wait_ge(s_pv, NSTEP * b + max(k - 1, 0))
                for p in range(2):
                    act.wait_ge(s_sc, NPAIR * b + 2 * k + p + 1)
                    nc.scalar.activation(probs[:, k % 2, 2 * p:2 * p + 2, 0:wd], ps_s[:, 2 * p:2 * p + 2, 0:wd],
                                         ACT.Exp, scale=LOGIT_SCALE).then_inc(s_p, 1)

            def copy_out(b, n):
                act.wait_ge(s_pv, NSTEP * b + GROUP_END[n] + 1)
                act.wait_ge(s_ot, NGRP * b + max(n - 1, 0))
                nc.scalar.copy(out_t[:, n % 2], ps_o[:]).then_inc(s_oc, 1)

            def take_turned(b):
                for j in range(1, TILES, 2):
                    act.wait_ge(s_turned, TILES * b + j + 1)
                    act.wait_ge(s_sc, NPAIR * b)
                    nc.scalar.copy(hidden_t[:, j, P * j:S], turn_banks[j % 4][:, 0:S - P * j]).then_inc(s_hid[1], 1)

            def batch(b, more):
                if more:
                    for c in range(EARLY):
                        keep_positive(b + 1, c)
                take_turned(b)
                exponents(b, 0)
                for k in range(NSTEP):
                    if k + 1 < NSTEP:
                        exponents(b, k + 1)
                    if k in GROUP_END:
                        copy_out(b, GROUP_END.index(k))
                    if more:
                        for c in CHUNKS_AT[k]:
                            keep_positive(b + 1, c)

            for c in range(NCHUNK):
                keep_positive(0, c)
            with act.Fori(0, B - 1) as b:
                batch(b, True)
            batch(B - 1, False)

        @block.gpsimd
        def _(pool):
            link, restart, step = chain_on(pool, s_chp)
            link(nc.gpsimd.memset(v_op[:, :, :, DK:VW], 0.0))
            link(nc.gpsimd.memset(k_op[64:KC], 1.0))
            link(nc.gpsimd.memset(q_op[64:KC], 0.0))
            nc.gpsimd.memset(v_op[:, :, :, DK:DK + 1], 1.0).then_inc(s_init, 1)
            pool.wait_ge(s_init, 1)
            pool.wait_ge(s_sqb, 1)
            nc.gpsimd.tensor_tensor(bound[:, 2:3], bound[:, 0:1], bound[:, 1:2], ALU.pow).then_inc(s_root, 1)

            def combine(n):
                restart()
                link(nc.gpsimd.tensor_copy(iw_cur[:], iw_all[:, bass.ds(TILES * n, TILES), :]))
                for c, (i, c0, wd, h) in enumerate(CHUNKS):
                    dst = index[:, i % 2, c0:c0 + wd]
                    weight = iw_cur[:, i, h:h + 1]
                    if h == 0 and c0 == 0 and (i >= 2 or not isinstance(n, int)):
                        pool.wait_ge(s_sel, TILES * n + i - 1)
                    pool.wait_ge(s_relu, NCHUNK * n + c + 1)
                    step()
                    r = relu[:, c % 4, 0:wd]
                    if h == 0:
                        last = nc.gpsimd.tensor_scalar(dst, r, weight, 0.0, ALU.mult, ALU.add)
                    else:
                        link(nc.gpsimd.tensor_scalar(r, r, weight, 0.0, ALU.mult, ALU.add))
                        pool.wait_ge(s_relu_used, NCHUNK * n + c)
                        last = nc.gpsimd.tensor_tensor(dst, dst, r, ALU.add)
                    last.then_inc(s_relu_used, 1)
                    if h == IH - 1 and c0 + wd == P * (i + 1):
                        diag = index[:, i % 2, P * i:P * (i + 1)]
                        pool.wait_ge(s_relu_used, NCHUNK * n + c + 1)
                        step()
                        nc.gpsimd.affine_select(out=diag, in_=diag, compare_op=ALU.is_ge, fill=NOT_CAUSAL, base=0,
                                                pattern=[[-1, P]], channel_multiplier=1).then_inc(s_index, 1)

            def place_values(b):
                pool.wait_ge(s_pv, NSTEP * b)
                pool.wait_ge(s_init, 1)
                nc.gpsimd.tensor_copy(v_op[:, :, :, 0:DK],
                                      v_all[:, bass.ds(TILES * b, TILES), :].rearrange("p j (h d) -> p j h d", h=HEADS)
                                      ).then_inc(s_v, 1)

            def store(b):
                pool.wait_ge(s_norm, NGRP * b + NGRP)
                pool.dma_start(t["rows"][b], rows_out[:]).then_inc(s_st, 16)

            combine(0)
            with pool.Fori(0, B - 1) as b:
                place_values(b)
                combine(b + 1)
                store(b)
            place_values(B - 1)
            store(B - 1)

        @block.vector
        def _(dve):
            link, restart, _ = chain_on(dve, s_chv)
            link_max, restart_max, _ = chain_on(dve, s_chm)

            def select(n, i, take=None):
                wd = P * (i + 1)
                cur = index[:, i % 2, 0:P * (i + 1)]
                for found in range(ROUNDS):
                    if take:
                        take(i, found)
                    if found == 0:
                        dve.wait_ge(s_index, TILES * n + i + 1)
                        link(nc.vector.memset(best[:], 0.0))
                    link(nc.vector.max(best[:], cur))
                    link(nc.vector.match_replace(cur, best[:], cur, TAKEN))
                nc.vector.tensor_scalar(hidden[:, i, 0:P * (i + 1)], cur, TAKEN, HIDE, ALU.is_gt,
                                        ALU.mult).then_inc(s_sel, 1)
                if take:
                    take(i, ROUNDS)

            def take_turned(b):
                for j in range(0, TILES, 2):
                    dve.wait_ge(s_turned, TILES * b + j + 1)
                    dve.wait_ge(s_sc, NPAIR * b)
                    nc.vector.tensor_copy(hidden_t[:, j, P * j:S],
                                          turn_banks[j % 4][:, 0:S - P * j]).then_inc(s_hid[0], 1)

            def maxima(b, hg):
                restart_max()
                for m in range(NMAX):
                    i = m // HL
                    dve.wait_ge(s_ms, NMAX * (HG * b + hg) + m + 1)
                    if P * (i + 1) <= BANK:
                        src, axis = ps_s[:, 2 * (m % 2), 0:P * (i + 1)], AX.X
                    else:
                        src = ps_s[:].rearrange("p c t -> p (c t)")[:, 2 * BANK * (m % 2):2 * BANK * (m % 2) + P * (i + 1)]
                        axis = AX.X
                    last = nc.vector.tensor_reduce(top[:, TILES * (m % HL) + i:TILES * (m % HL) + i + 1], src, axis, ALU.max)
                    last.then_inc(s_mt, 1)
                dve.wait_ge(s_mt, NMAX * (HG * b + hg + 1))
                dve.sem_inc(s_mtop, 1)
                dve.wait_ge(s_mturn, HG * b + hg + 1)
                if not (isinstance(b, int) and b == 0 and hg == 0):
                    dve.wait_ge(s_cl, 32 + 16 * PARTS * (HG * b + hg))
                link_max(nc.vector.tensor_scalar(neg[:, 0], ps_s[0:NMAX, 0, 0:P], -1.0, None, ALU.mult))
                link_max(nc.vector.tensor_copy(neg_parts[:, 0], neg[:, 0]))
                link_max(nc.vector.tensor_tensor(neg[:, 1], neg[:, 0], neg_parts[:, 0], ALU.subtract))
                link_max(nc.vector.tensor_copy(neg_parts[:, 1], neg[:, 1]))
                nc.vector.tensor_tensor(neg_parts[:, 2], neg[:, 1], neg_parts[:, 1],
                                        ALU.subtract).then_inc(s_neg, 1)

            def normalise(b, n):
                hg, g = n // GROUPS, n % GROUPS
                dve.wait_ge(s_ot, NGRP * b + n + 1)
                if n == 0 and not (isinstance(b, int) and b == 0):
                    dve.wait_ge(s_st, 16 * b)
                src = ps_t[:].rearrange("p (c h v) -> p c h v", c=4, h=HL)
                link(nc.vector.reciprocal(recip[:], src[:, :, :, DK]))
                dst = rows_out[:, 4 * g:4 * g + 4, 32 * hg:32 * hg + 32].rearrange("p c (h d) -> p c h d", h=HL)
                rb = recip[:].rearrange("p c (h o) -> p c h o", o=1).broadcast_to([P, 4, HL, DK])
                nc.vector.tensor_tensor(dst, src[:, :, :, 0:DK], rb, ALU.mult).then_inc(s_norm, 1)

            def batch(b, more):
                restart()
                take_turned(b)

                def take(i, found):
                    for what, n in EVENTS.get((i, found), []):
                        if what == "norm":
                            normalise(b, n)
                        else:
                            with dve.If(exact > 0):
                                maxima(b, n)

                for i in range(TILES):
                    if more:
                        select(b + 1, i, take)
                    else:
                        for found in range(ROUNDS + 1):
                            take(i, found)

            link(nc.vector.tensor_reduce(peaks[:], peak[:], AX.X, ALU.max))
            nc.vector.tensor_tensor(peak_product[:], peaks[:, 0:1], peaks[:, 1:2], ALU.mult).then_inc(s_pk, 1)
            link(nc.vector.memset(shift_row[:], 0.0))
            link(nc.vector.memset(bound[:, 1:2], 0.5))
            dve.wait_ge(s_hb, 1)
            nc.vector.tensor_reduce(bound[:, 0:1], ps_t[0:1, 0:HEADS], AX.X, ALU.max).then_inc(s_sqb, 1)
            dve.wait_ge(s_sqb, 1)
            link(nc.vector.tensor_scalar(exact_flag[:], bound[:, 0:1], (SAFE / LOGIT_SCALE) ** 2, None, ALU.is_gt))
            dve.wait_ge(s_root, 1)
            link(nc.vector.tensor_scalar(bound[:, 3:4], bound[:, 2:3], -1.01, None, ALU.mult))
            nc.vector.tensor_scalar(shift_row[:], shift_row[:], bound[:, 3:4], None, ALU.add).then_inc(s_bd, 1)
            dve.wait_ge(s_bd, 1)
            exact = dve.value_load(exact_flag[0:1, 0:1], min_val=0, max_val=1)
            for i in range(TILES):
                select(0, i)
            with dve.Fori(0, B - 1) as b:
                batch(b, True)
            batch(B - 1, False)


def finish_all(nc, t):
    with ExitStack() as ctx:
        def sb(name, shape, dt):
            return ctx.enter_context(nc.sbuf_tensor(name, shape, dt))

        def sem(name):
            return ctx.enter_context(nc.semaphore(name))

        NT = BANK // P
        NH = STATE // P
        ident = sb("identF", [P, P], F32)
        wo = sb("wo", [P, D], F32)
        w1 = sb("w1", [P, STATE], F32)
        w2 = sb("w2", [P, NH, D], F32)
        b1 = sb("b1", [P, NH], F32)
        b2 = sb("b2", [P, D], F32)
        xs = sb("xf", [P, 2, NT, D], F32)
        orow = sb("orow", [P, 2, NT, D], F32)
        oT = sb("oTf", [P, BANK], F32)
        x2 = sb("x2", [P, 2, NT, D], F32)
        stats = sb("statsf", [P, NT, 6], F32)
        mv = sb("mvf", [P, NT, 2], F32)
        var = sb("varf", [P, NT], F32)
        power = sb("powerf", [P, NT], F32)
        rstd = sb("rstdf", [P, NT], F32)
        xn = sb("xnf", [P, NT, D], F32)
        xT = sb("xTf", [P, BANK], F32)
        h = sb("h", [P, NH, BANK], F32)
        res = sb("res", [P, 2, NT, D], F32)
        ps = ctx.enter_context(nc.psum_tensor("psf", [P, 8, BANK], F32))

        s_w = sem("ffn_weights_loaded")
        s_x = [sem(f"rows_loaded{e}") for e in range(2)]
        s_ot = sem("attn_turned")
        s_oT = sem("attn_t_copied")
        s_pr = sem("attn_projected")
        s_x2 = sem("x2_ready")
        s_pow = sem("power2_filled")
        s_var = sem("variances2_ready")
        s_rstd = sem("rstd2_ready")
        s_xn = sem("xn2_ready")
        s_t = sem("xn2_turned")
        s_xT = sem("xn2_t_copied")
        s_h = sem("hidden_products")
        s_g = sem("gelu_done")
        s_y = sem("ffn_products")
        s_res = sem("result_ready")
        s_st = sem("result_stored")
        s_ch = sem("vector_chain_f")
        block = ctx.enter_context(nc.Block())

        @block.sync
        def _(sp):
            def load(b, half):
                sp.dma_start(orow[:, half], t["rows"][b, :, NT * half:NT * (half + 1)]).then_inc(s_x[half], 16)
                sp.dma_start(xs[:, half], t["x"][b, half]).then_inc(s_x[half], 16)

            sp.dma_start(ident[:], t["ident"]).then_inc(s_w, 16)
            load(0, 0)
            for dst, name in ((wo, "wo"), (w1, "w1"), (b1, "b1"), (w2, "w2"), (b2, "b2")):
                sp.dma_start(dst[:], t[name]).then_inc(s_w, 16)
            load(0, 1)

            def batch(b, more):
                for half in range(2):
                    n = 2 * b + half
                    if more:
                        sp.wait_ge(s_x2, n + 1)
                        load(b + 1, half)
                    sp.wait_ge(s_res, n + 1)
                    sp.dma_start(t["out"][b, half], res[:, half]).then_inc(s_st, 16)

            with sp.Fori(0, B - 1) as b:
                batch(b, True)
            batch(B - 1, False)
            sp.wait_ge(s_st, 16 * 2 * B)

        @block.tensor
        def _(pe):
            def turn_attn(b, half):
                n = 2 * b + half
                pe.wait_ge(s_x[half], 32 * b + 32)
                pe.wait_ge(s_oT, n)
                for j in range(NT):
                    last = nc.tensor.transpose(ps[:, 0, P * j:P * (j + 1)], orow[:, half, j], ident[:])
                last.then_inc(s_ot, 1)

            def project(n):
                pe.wait_ge(s_x2, n)
                pe.wait_ge(s_oT, n + 1)
                for j in range(NT):
                    last = nc.tensor.matmul(ps[:, 1, P * j:P * (j + 1)], oT[:, P * j:P * (j + 1)], wo[:],
                                            start=True, stop=True)
                last.then_inc(s_pr, 1)

            def turn_xn(n):
                pe.wait_ge(s_xT, n)
                pe.wait_ge(s_xn, n + 1)
                for j in range(NT):
                    last = nc.tensor.transpose(ps[:, 2, P * j:P * (j + 1)], xn[:, j], ident[:])
                last.then_inc(s_t, 1)

            def batch(b, more):
                for half in range(2):
                    n = 2 * b + half
                    pe.wait_ge(s_g, NH * n)
                    pe.wait_ge(s_xT, n + 1)
                    for m in range(NH):
                        nc.tensor.matmul(ps[:, 3 + m], w1[:, P * m:P * (m + 1)], xT[:], start=True,
                                         stop=True).then_inc(s_h, 1)
                    if more:
                        turn_attn(b + 1, half)
                    if half == 0 or more:
                        turn_xn(n + 1)
                    if more:
                        project(n + 2)
                    pe.wait_ge(s_res, n)
                    pe.wait_ge(s_g, NH * n + NH)
                    for j in range(NT):
                        for m in range(NH):
                            last = nc.tensor.matmul(ps[:, 7, P * j:P * (j + 1)], h[:, m, P * j:P * (j + 1)],
                                                    w2[:, m], start=(m == 0), stop=(m == NH - 1))
                    last.then_inc(s_y, 1)

            pe.wait_ge(s_w, 96)
            for half in range(2):
                turn_attn(0, half)
                project(half)
            turn_xn(0)
            with pe.Fori(0, B - 1) as b:
                batch(b, True)
            batch(B - 1, False)

        @block.scalar
        def _(act):
            def copy_attn(n):
                act.wait_ge(s_pr, n)
                act.wait_ge(s_ot, n + 1)
                nc.scalar.copy(oT[:], ps[:, 0]).then_inc(s_oT, 1)

            def copy_xn(n):
                act.wait_ge(s_h, NH * n)
                act.wait_ge(s_t, n + 1)
                nc.scalar.copy(xT[:], ps[:, 2]).then_inc(s_xT, 1)

            def batch(b, more):
                for half in range(2):
                    n = 2 * b + half
                    act.wait_ge(s_y, n)
                    for m in range(NH):
                        act.wait_ge(s_h, NH * n + m + 1)
                        nc.scalar.activation(h[:, m], ps[:, 3 + m], ACT.Gelu, bias=b1[:, m:m + 1]).then_inc(s_g, 1)
                    if more:
                        copy_attn(n + 2)
                    if half == 0 or more:
                        copy_xn(n + 1)

            act.wait_ge(s_w, 96)
            copy_attn(0)
            copy_attn(1)
            copy_xn(0)
            with act.Fori(0, B - 1) as b:
                batch(b, True)
            batch(B - 1, False)

        @block.gpsimd
        def _(pool):
            nc.gpsimd.memset(power[:], -0.5).then_inc(s_pow, 1)
            pool.wait_ge(s_pow, 1)
            with pool.Fori(0, 2 * B) as n:
                pool.wait_ge(s_var, n + 1)
                pool.wait_ge(s_xn, n)
                nc.gpsimd.tensor_tensor(rstd[:], var[:], power[:], ALU.pow).then_inc(s_rstd, 1)

        @block.vector
        def _(dve):
            link, restart, _ = chain_on(dve, s_ch)

            def residual_and_norm(b, half):
                n = 2 * b + half
                if not isinstance(n, int):
                    dve.wait_ge(s_res, n - 1)
                dve.wait_ge(s_x[half], 32 * b + 32)
                dve.wait_ge(s_pr, n + 1)
                nc.vector.tensor_tensor(x2[:, half].rearrange("p j d -> p (j d)"), ps[:, 1],
                                        xs[:, half].rearrange("p j d -> p (j d)"), ALU.add).then_inc(s_x2, 1)
                dve.wait_ge(s_x2, n + 1)
                for j in range(NT):
                    link(nc.vector.bn_stats(stats[:, j], x2[:, half, j]))
                for j in range(NT):
                    link(nc.vector.bn_aggr(mv[:, j], stats[:, j]))
                nc.vector.tensor_scalar(var[:], mv[:, :, 1], EPS, None, ALU.add).then_inc(s_var, 1)
                dve.wait_ge(s_rstd, n + 1)
                dve.wait_ge(s_t, n)
                for j in range(NT):
                    last = nc.vector.tensor_scalar(xn[:, j], x2[:, half, j], mv[:, j, 0:1], rstd[:, j:j + 1],
                                                   ALU.subtract, ALU.mult)
                last.then_inc(s_xn, 1)
                dve.wait_ge(s_xn, n + 1)
                b2v = b2[:].rearrange("p (o d) -> p o d", o=1).broadcast_to([P, NT, D])
                link(nc.vector.tensor_tensor(x2[:, half], x2[:, half], b2v, ALU.add))

            def batch(b, more):
                restart()
                for half in range(2):
                    n = 2 * b + half
                    dve.wait_ge(s_y, n + 1)
                    dve.wait_ge(s_st, 32 * b)
                    nc.vector.tensor_tensor(res[:, half].rearrange("p j d -> p (j d)"), ps[:, 7],
                                            x2[:, half].rearrange("p j d -> p (j d)"), ALU.add).then_inc(s_res, 1)
                    if more:
                        residual_and_norm(b + 1, half)

            dve.wait_ge(s_w, 96)
            residual_and_norm(0, 0)
            residual_and_norm(0, 1)
            with dve.Fori(0, B - 1) as b:
                batch(b, True)
            batch(B - 1, False)


def build(nc, t):
    with ExitStack() as ctx:
        v_all = ctx.enter_context(nc.sbuf_tensor("v_all", [P, B * TILES, P], F32))
        iw_all = ctx.enter_context(nc.sbuf_tensor("iw_all", [P, B * TILES, IH], F32))
        peak = ctx.enter_context(nc.sbuf_tensor("peak", [HEADS, 2, 2 * B], F32))
        project_all(nc, t, v_all, iw_all, peak)
        attend_all(nc, t, v_all, iw_all, peak)
        finish_all(nc, t)


def kernel(**inputs):
    import ml_dtypes
    import numpy as np
    import concourse.bacc as bacc
    from concourse.bass_utils import run_bass_kernel_spmd

    order = np.array([(hg * HL + hl) * DK + d for hg in range(HG) for d in range(DK) for hl in range(HL)])
    swap = order ^ 1
    qkv = np.asarray(inputs["L0_attn_qkv_w"])
    wq, wk, wv = qkv[0:D], qkv[D:2 * D], qkv[2 * D:3 * D]
    w = np.concatenate([wq[order], wq[swap], wk[order], wk[swap], np.asarray(inputs["L0_attn_iq_w"]),
                        np.asarray(inputs["L0_attn_ik_w"]), wv, np.asarray(inputs["L0_attn_iw_w"])], axis=0)
    w = np.ascontiguousarray(w.T)
    f32 = np.float32
    inv = (f32(1.0) / np.power(f32(1250.0), np.arange(0, DK, 2, dtype=f32) / f32(DK))).astype(f32)
    freqs = np.outer(np.arange(S, dtype=f32), inv).astype(f32)
    ch = order % DK
    cos = np.ascontiguousarray(np.cos(freqs)[:, ch // 2].T.astype(f32))
    sin = np.ascontiguousarray((np.sin(freqs)[:, ch // 2] * np.where(ch % 2 == 0, -1.0, 1.0)).T.astype(f32))
    eye = np.eye(P, dtype=f32)
    head_of = np.zeros((P, HEADS), ml_dtypes.bfloat16)
    head_of[np.arange(P), order // DK] = 1.0
    given = {
        "head_of": head_of,
        "x": np.asarray(inputs["L0_attn_x"]),
        "w": w, "cos": cos, "sin": sin, "ident": eye, "identb": eye.astype(ml_dtypes.bfloat16),
        "wo": np.ascontiguousarray(np.asarray(inputs["L0_attn_wo_w"]).T),
        "w1": np.asarray(inputs["L0_ffn_w1"]), "w2": np.asarray(inputs["L0_ffn_w2"]),
        "b1": np.asarray(inputs["L0_ffn_b1"]).reshape(STATE // P, P).T, "b2": np.asarray(inputs["L0_ffn_b2"]),
    }
    nc = bacc.Bacc("TRN2", target_bir_lowering=False, num_devices=1)
    t = {}
    arrays = {}
    for name, a in given.items():
        a = np.ascontiguousarray(a)
        arrays["in_" + name] = a
        t[name] = nc.dram_tensor("in_" + name, a.shape, mybir.dt.from_np(a.dtype), kind="ExternalInput").ap()
    NT = BANK // P
    t["x"] = t["x"].rearrange("b (g j p) d -> b g p j d", g=2, p=P)
    t["w2"] = t["w2"].rearrange("(m p) d -> p m d", p=P)
    t["b2"] = t["b2"].rearrange("(o d) -> o d", o=1).broadcast_to([P, D])
    for name in ("q", "k", "iq0", "iq1", "ik"):
        rows = ID if name == "ik" else P
        t[name + "_parts"] = nc.dram_tensor(name + "_parts", (B, PARTS, rows, S), BF16, kind="Internal").ap()
    t["rows"] = nc.dram_tensor("attn_rows", (B, P, TILES, D), F32, kind="Internal").ap()
    out = nc.dram_tensor("out_0", (B, S, D), F32, kind="ExternalOutput").ap()
    t["out"] = out.rearrange("b (g j p) d -> b g p j d", g=2, p=P)
    build(nc, t)
    r = run_bass_kernel_spmd(nc, [arrays], core_ids=[0])
    return r.results[0]["out_0"]
```

```python
from contextlib import ExitStack

import concourse.bass as bass
from concourse import mybir

F32 = mybir.dt.float32
BF16 = mybir.dt.bfloat16
ALU = mybir.AluOpType
ACT = mybir.ActivationFunctionType
AX = mybir.AxisListType

P = 128
BANK = 512
B, S, D = 4, 1024, 128
HEADS, DK = 16, 8
IH, ID = 4, 64
TOPK = 64
STATE = 512
HG, HL = 4, 4
TILES = S // P
GROUPS = S // BANK
PARTS = 3
KROWS = PARTS * PARTS * DK
KC = KROWS + PARTS
VW = 32
EPS = 1e-5
NOT_CAUSAL = -1.0e9
TAKEN = -3.0e38
HIDE = -1.0e30
SAFE = 40.0
LOGIT_SCALE = float(DK) ** -0.5

STEPS = [(hg, g, j) for hg in range(HG) for g in range(GROUPS) for j in range(4 * g + 4)]
CHUNKS = [(i, c, min(BANK, P * (i + 1) - c), h)
          for i in range(TILES) for c in range(0, P * (i + 1), BANK) for h in range(IH)]
NSTEP, NCHUNK, NPAIR = len(STEPS), len(CHUNKS), 2 * len(STEPS)
assert NSTEP == NCHUNK == 48
NGRP = HG * GROUPS
HALF_CHUNKS = 16
GROUP_END = [k for k in range(NSTEP) if k + 1 == NSTEP or STEPS[k + 1][:2] != STEPS[k][:2]]


def span(k):
    _, g, j = STEPS[k]
    t0 = max(P * j, BANK * g)
    return t0, BANK * (g + 1) - t0


ROUNDS = TOPK // 8
PAIRS = TILES // 2
PB = 3
UNMASKED = 1
RING = 4
EARLY = 2 * IH
PAIR_COST = [2 * (2 * p + 1) + 3.0 for p in range(PAIRS)]
COST_SUM = sum(PAIR_COST)


def windows(first, last):
    return [first + (last - first) * sum(PAIR_COST[:p]) / COST_SUM for p in range(PAIRS + 1)]


def chunk_times(start, lead):
    times = []
    for c, (i, _, _, _) in enumerate(CHUNKS):
        p = i // 2
        mine = [x for x, ch in enumerate(CHUNKS) if ch[0] // 2 == p]
        share = (c - mine[0]) / len(mine)
        times.append(max(0.0, start[p - 1] - lead + (start[p] - start[p - 1]) * 0.85 * share) if p else -1.0)
    return times


NTURN = 6
NEXT_TURNS = {41: 0, 43: 1}
TURNS = {0: (2, 3), 1: (4, 5)}
EARLY_AT = {0: range(0, 3), 1: range(3, 6), 2: range(6, EARLY)}


def turned_blocks(v):
    g = int(v >= 2)
    return [(j, max(4 * g, j), 4 * g + 4) for j in (2 * v - 4 * g, 2 * v - 4 * g + 1)]


def plan_batch():
    wide = [span(k)[1] for k in range(NSTEP)]
    done = [sum(wide[:k + 1]) / sum(wide) for k in range(NSTEP)]
    start = windows(0.0, 0.955)
    chunks_at = [[] for _ in range(NSTEP)]
    for c, aim in enumerate(chunk_times(start, 0.02)):
        if aim >= 0.0:
            chunks_at[max(len(EARLY_AT), next(k for k in range(NSTEP) if done[k] >= aim))].append(c)
    events = {}
    todo = [(done[k + 1] if k + 1 < NSTEP else 2.0, "norm", n) for n, k in enumerate(GROUP_END)]
    todo += [(done[GROUP_END[n - 1] - 1] if n else -1.0, "max", n) for n in range(NGRP)]
    todo += [(done[k], "turn", v) for k, v in NEXT_TURNS.items() if v == 0]
    for when, what, n in sorted(todo):
        p = max([x for x in range(PAIRS) if start[x] <= when], default=0)
        r = int(ROUNDS * max(when - start[p], 0) / (start[p + 1] - start[p]))
        events.setdefault((p, min(ROUNDS, r)), []).append((what, n))
    return chunks_at, events


SLOTS = 4
FIRST = 2


def plan_first():
    slots = SLOTS * (GROUPS * B + 1 - FIRST)
    start = windows(0.05, 0.90)
    chunks_at = [[] for _ in range(slots)]
    for c, aim in enumerate(chunk_times(start, 0.0)):
        chunks_at[max(1, min(slots - 1, int(aim * slots + 1)))].append(c)
    rounds_at = [[] for _ in range(slots)]
    for p in range(PAIRS):
        for r in range(ROUNDS):
            when = start[p] + (start[p + 1] - start[p]) * r / ROUNDS
            rounds_at[min(slots - 1, int(when * slots + 1))].append((p, r))
    return chunks_at, rounds_at


CHUNKS_AT, EVENTS = plan_batch()
FIRST_CHUNKS, FIRST_ROUNDS = plan_first()
QK_DMAS = 3 + 5
INDEX_DMAS = 6 + 4


class Chain:

    def __init__(self, eng, sem):
        self.eng, self.sem, self.count = eng, sem, 0

    def mark(self, ins):
        self.count += 1
        ins.then_inc(self.sem, 1)

    def wait(self, behind=0):
        if self.count > behind:
            self.eng.wait_ge(self.sem, self.count - behind)

    def link(self, ins):
        self.mark(ins)
        self.wait()

    def step(self):
        self.count += 1
        self.eng.sem_inc(self.sem, 1)
        self.wait()

    def restart(self):
        self.count = 0
        self.eng.sem_clear(self.sem)


class Selection:

    def __init__(self, nc, ctx, iw_all):
        def sb(name, shape, dt):
            return ctx.enter_context(nc.sbuf_tensor(name, shape, dt))

        def sem(name):
            return ctx.enter_context(nc.semaphore(name))

        self.nc = nc
        self.iw_all = iw_all
        self.iq_op = sb("iq_op", [P, 2, 3, IH, BANK], BF16)
        self.ik_op = sb("ik_op", [P, 2, 2, S], BF16)
        self.iw_cur = sb("iw_cur", [P, TILES, IH], F32)
        self.relu = sb("relu", [P, 4, BANK], F32)
        self.index = sb("index", [P, RING, S], F32)
        self.best = sb("best", [P, 2, 8], F32)
        self.hidden = sb("hidden", [P, TILES, S], BF16)
        self.dots_ps = ctx.enter_context(nc.psum_tensor("dots_ps", [P, 2, BANK], F32))
        self.s_iqk = [sem(f"index_operands_loaded{r}") for r in range(2)]
        self.s_dots = sem("dots_ready")
        self.s_relu = sem("relu_ready")
        self.s_relu_used = sem("relu_used")
        self.s_weighed = sem("scores_weighed")
        self.s_index = sem("index_ready")
        self.s_sel = sem("selected")

    def load(self, sp, t, b):
        for half in range(2):
            n = BANK * (half + 1)
            for combo, pair in enumerate(((0, 0), (1, 1), (0, 2))):
                for lo, part in enumerate(pair):
                    src = t["iq_parts"][b, part, :, :, BANK * half:BANK * (half + 1)]
                    sp.dma_start(self.iq_op[ID * lo:ID * lo + ID, half, combo],
                                 src.rearrange("h d t -> d h t")).then_inc(self.s_iqk[half], 16)
            for combo, pair in enumerate(((0, 1), (2, 0))):
                for lo, part in enumerate(pair):
                    sp.dma_start(self.ik_op[ID * lo:ID * lo + ID, half, combo, 0:n],
                                 t["ik_parts"][b, part, :, 0:n]).then_inc(self.s_iqk[half], 16)

    def dots(self, pe, n, c):
        i, c0, wd, h = CHUNKS[c]
        half = i // 4
        if c == 0:
            pe.wait_ge(self.s_iqk[0], 16 * INDEX_DMAS * n + 16 * INDEX_DMAS)
        if c == HALF_CHUNKS:
            pe.wait_ge(self.s_iqk[1], 16 * INDEX_DMAS * n + 16 * INDEX_DMAS)
        if c >= 2 or not isinstance(n, int):
            pe.wait_ge(self.s_relu, NCHUNK * n + c - 1)
        qc = slice(P * (i % 4), P * (i % 4) + P)
        for m, kc in enumerate((0, 0, 1)):
            last = self.nc.tensor.matmul(self.dots_ps[:, c % 2, 0:wd], self.iq_op[:, half, m, h, qc],
                                         self.ik_op[:, half, kc, c0:c0 + wd], start=(m == 0), stop=(m == 2))
        last.then_inc(self.s_dots, 1)

    def keep_positive(self, act, n, c):
        i, c0, wd, h = CHUNKS[c]
        act.wait_ge(self.s_dots, NCHUNK * n + c + 1)
        if c >= 4 or not isinstance(n, int):
            act.wait_ge(self.s_relu_used, NCHUNK * n + c - 3)
        r = self.relu[:, c % 4, 0:wd]
        self.nc.scalar.activation(r, self.dots_ps[:, c % 2, 0:wd], ACT.Relu).then_inc(self.s_relu, 1)
        if self.weighed_by_act(n):
            act.wait_ge(self.s_relu, c + 1)
            self.nc.scalar.activation(r, r, ACT.Copy, scale=self.iw_all[:, i, h:h + 1]).then_inc(self.s_weighed, 1)

    def weighed_by_act(self, n):
        return isinstance(n, int) and n == 0

    def begin_combine(self, chain, n):
        chain.restart()
        chain.link(self.nc.gpsimd.tensor_copy(self.iw_cur[:], self.iw_all[:, bass.ds(TILES * n, TILES), :]))

    def combine(self, pool, chain, n, c):
        nc = self.nc
        i, c0, wd, h = CHUNKS[c]
        dst = self.index[:, i % RING, c0:c0 + wd]
        weight = self.iw_cur[:, i, h:h + 1]
        if h == 0 and c0 == 0 and (i >= RING or not isinstance(n, int)):
            pool.wait_ge(self.s_sel, TILES * n + i - RING + 1)
        r = self.relu[:, c % 4, 0:wd]
        if self.weighed_by_act(n):
            if h:
                pool.wait_ge(self.s_weighed, c + 1)
                if h > 1:
                    pool.wait_ge(self.s_relu_used, c)
                term = self.relu[:, (c - 1) % 4, 0:wd] if h == 1 else dst
                nc.gpsimd.tensor_tensor(dst, term, r, ALU.add).then_inc(self.s_relu_used, 2 if h == 1 else 1)
        else:
            pool.wait_ge(self.s_relu, NCHUNK * n + c + 1)
            chain.step()
            if h == 0:
                last = nc.gpsimd.tensor_scalar(dst, r, weight, 0.0, ALU.mult, ALU.add)
            else:
                chain.link(nc.gpsimd.tensor_scalar(r, r, weight, 0.0, ALU.mult, ALU.add))
                pool.wait_ge(self.s_relu_used, NCHUNK * n + c)
                last = nc.gpsimd.tensor_tensor(dst, dst, r, ALU.add)
            last.then_inc(self.s_relu_used, 1)
        if h == IH - 1 and c0 + wd == P * (i + 1):
            diag = self.index[:, i % RING, P * i:P * (i + 1)]
            pool.wait_ge(self.s_relu_used, NCHUNK * n + c + 1)
            chain.step()
            nc.gpsimd.affine_select(out=diag, in_=diag, compare_op=ALU.is_ge, fill=NOT_CAUSAL, base=0,
                                    pattern=[[-1, P]], channel_multiplier=1).then_inc(self.s_index, 1)

    def select(self, dve, chain, n, p, r):
        nc = self.nc
        tiles = [(e, 2 * p + e, self.index[:, (2 * p + e) % RING, 0:P * (2 * p + e + 1)]) for e in range(2)]
        if r == 0:
            dve.wait_ge(self.s_index, TILES * n + 2 * p + 2)
            chain.step()
        for e, i, scores in tiles:
            chain.wait(behind=1)
            chain.mark(nc.vector.max(self.best[:, e], scores))
        for e, i, scores in tiles:
            chain.wait(behind=1)
            chain.mark(nc.vector.match_replace(scores, self.best[:, e], scores, TAKEN))
        if r == ROUNDS - 1:
            for e, i, scores in tiles:
                chain.wait(behind=1 - e)
                nc.vector.tensor_scalar(self.hidden[:, i, 0:P * (i + 1)], scores, TAKEN, HIDE, ALU.is_gt,
                                        ALU.mult).then_inc(self.s_sel, 1)


def load_head_group(sp, t, q_op, k_op, s_qk, b, hg):
    r = hg % 2
    rows = slice(32 * hg, 32 * hg + 32)
    q = t["q_parts"][b, :, rows, :].rearrange("p (d h) t -> p d (h t)", h=HL)
    k = t["k_parts"][b, :, rows, :].rearrange("p (d h) t -> p d (h t)", h=HL)
    G = PARTS * DK
    for rep in range(PARTS):
        sp.dma_start(q_op[G * rep:G * rep + G, r].rearrange("p h t -> p (h t)"), q).then_inc(s_qk[r], 16)
        cut = DK * (PARTS - rep)
        sp.dma_start(k_op[G * rep:G * rep + cut, r].rearrange("p h t -> p (h t)"), k[rep:]).then_inc(s_qk[r], 16)
        if rep:
            sp.dma_start(k_op[G * rep + cut:G * rep + G, r].rearrange("p h t -> p (h t)"),
                         k[:rep]).then_inc(s_qk[r], 16)


def project_and_select_first(nc, t, ident, identb, sel, v_all, iw_all, q_op, k_op, bound, s_init, s_qk):
    with ExitStack() as ctx:
        def sb(name, shape, dt):
            return ctx.enter_context(nc.sbuf_tensor(name, shape, dt))

        def sem(name):
            return ctx.enter_context(nc.semaphore(name))

        NT = BANK // P
        NA = GROUPS * B
        NW = 7 * P + IH
        COL = dict(q=0, qs=P, k=2 * P, ks=3 * P, iq0=4 * P, iq1=5 * P, ik=6 * P, v=6 * P + ID)
        w = sb("w", [P, NW + ID], F32)
        cos = sb("cos", [P, S], F32)
        sin = sb("sin", [P, S], F32)
        power = sb("power", [P, NT], F32)
        head_of = sb("head_of", [P, HEADS], BF16)
        squares = sb("squares", [P, 2, BANK], BF16)
        peak = sb("peak", [P, 2 * NT * HEADS], F32)
        peak2 = sb("peak2", [P, 2, HEADS], F32)
        peak_t = sb("peak_t", [HEADS, 2], F32)
        peak_product = sb("peak_product", [HEADS, 1], F32)
        xs = sb("xs", [P, 2, NT, D], F32)
        stats = sb("stats", [P, NT, 6], F32)
        mv = sb("mv", [P, NT, 2], F32)
        var = sb("var", [P, NT], F32)
        rstd = sb("rstd", [P, NT], F32)
        xn = sb("xn", [P, NT, D], F32)
        xT = sb("xT", [P, 3, BANK], F32)
        by_cos = sb("by_cos", [P, 2, BANK], F32)
        by_sin = sb("by_sin", [P, 2, BANK], F32)
        rot = sb("rot", [P, 2, BANK], F32)
        rest = sb("rest", [P, 5, BANK], F32)
        parts = sb("parts", [P, 5, PARTS, BANK], BF16)
        ps = ctx.enter_context(nc.psum_tensor("psx", [P, 6, BANK], F32))

        s_w = sem("weights_loaded")
        s_id = sem("identity_loaded")
        s_tab = sem("tables_loaded")
        s_x = [sem(f"x_loaded{h}") for h in range(2)]
        s_pow = sem("power_filled")
        s_var = sem("variances_ready")
        s_rstd = sem("rstd_ready")
        s_xn = sem("xn_ready")
        s_t = sem("xn_turned")
        s_xT = sem("xT_copied")
        s_mm = [sem("heads_projected"), sem("index_projected")]
        s_rc = sem("rope_products")
        s_rot = sem("rotated")
        s_sq = sem("squares_ready")
        s_nm = sem("norms_ready")
        s_peak = sem("peaks_taken")
        s_hi = [sem("high_parts_of_heads"), sem("high_parts_of_index")]
        s_rest = [sem("rests_of_heads_ready"), sem("rests_of_index_ready")]
        s_mid = [sem("middle_parts_of_heads"), sem("middle_parts_of_index")]
        s_lo = [sem("low_parts_of_heads"), sem("low_parts_of_index")]
        s_st = [sem("heads_stored"), sem("index_stored")]
        s_v = sem("values_copied")
        s_pt = sem("peaks_turned")
        s_pk = sem("peak_product_ready")
        s_hb = sem("head_bounds_ready")
        s_sqb = sem("squared_bound_ready")
        s_root = sem("bound_root_ready")
        s_chv = sem("vector_chain_a")
        s_cht = sem("selection_chain_a")
        s_chp = sem("pool_chain_a")
        block = ctx.enter_context(nc.Block())

        NHEAD, NINDEX = 4, 5
        SPLIT = ["q", "k", "iq0", "iq1", "ik"]
        BANK_OF = {"iq0": 5, "iq1": 0, "ik": 5}
        MADE = {"iq0": 1, "iq1": 2, "ik": 5}
        SIZE = (2, 3)

        def kind(a):
            return int(a >= 2)

        def upto(n, a):
            return SIZE[kind(a)] * n + (a - 1 if a >= 2 else a + 1)

        def before(n, a):
            return SIZE[kind(a)] * n

        def rows_of(a):
            return ID if SPLIT[a] == "ik" else P

        def whole(a):
            return rot[:, a] if a < 2 else ps[0:rows_of(a), BANK_OF[SPLIT[a]]]

        def slot(m, q):
            return SLOTS * (m - FIRST) + q if m >= FIRST else None

        @block.sync
        def _(sp):
            def load(n):
                sp.dma_start(xs[:, n % 2], t["x"][n // 2, n % 2]).then_inc(s_x[n % 2], 16)

            def store(n, a):
                cols = slice((n % 2) * BANK, (n % 2 + 1) * BANK)
                name = SPLIT[a]
                sp.wait_ge(s_mid[kind(a)], upto(n, a))
                sp.wait_ge(s_lo[kind(a)], upto(n, a))
                if name in ("iq0", "iq1"):
                    e = 2 * int(name == "iq1")
                    dst = t["iq_parts"][n // 2, :, e:e + 2, :, cols].rearrange("p h d t -> (h d) p t")
                else:
                    dst = t[name + "_parts"][n // 2, :, :, cols].rearrange("p c t -> c p t")
                sp.dma_start(dst, parts[0:rows_of(a), a]).then_inc(s_st[kind(a)], 16)

            load(0)
            sp.dma_start(ident[:], t["ident"]).then_inc(s_id, 16)
            sp.dma_start(w[:], t["w"]).then_inc(s_w, 16)
            load(1)
            sp.dma_start(cos[:], t["cos"]).then_inc(s_tab, 16)
            sp.dma_start(sin[:], t["sin"]).then_inc(s_tab, 16)
            sp.dma_start(head_of[:], t["head_of"]).then_inc(s_tab, 16)
            sp.dma_start(identb[:], t["identb"]).then_inc(s_tab, 16)
            for m in range(NA + 1):
                if m + 2 < NA:
                    sp.wait_ge(s_xn, m + 1)
                    load(m + 2)
                if m < NA:
                    for a in (2, 3, 4):
                        store(m, a)
                if m == FIRST - 1:
                    sp.wait_ge(s_st[1], 16 * SIZE[1] * FIRST)
                    sel.load(sp, t, 0)
                if m == NA - 1:
                    sp.wait_ge(s_st[1], 16 * SIZE[1] * 2 * FIRST)
                    sp.wait_ge(sel.s_dots, NCHUNK)
                    sel.load(sp, t, 1)
                if m:
                    for a in (0, 1):
                        store(m - 1, a)
                if m == FIRST:
                    sp.wait_ge(s_st[0], 16 * SIZE[0] * FIRST)
                    sp.wait_ge(s_init, 2)
                    load_head_group(sp, t, q_op, k_op, s_qk, 0, 0)
                    load_head_group(sp, t, q_op, k_op, s_qk, 0, 1)
            for e in range(2):
                sp.wait_ge(s_st[e], 16 * SIZE[e] * NA)

        @block.vector
        def _(dve):
            chain = Chain(dve, s_chv)
            picks = Chain(dve, s_cht)

            def fill(m, q):
                if slot(m, q) is not None:
                    for p, r in FIRST_ROUNDS[slot(m, q)]:
                        sel.select(dve, picks, 0, p, r)

            def moments(n):
                x = xs[:, n % 2]
                dve.wait_ge(s_x[n % 2], 16 * (n // 2) + 16)
                for j in range(NT):
                    chain.mark(nc.vector.bn_stats(stats[:, j], x[:, j]))
                chain.wait()
                for j in range(NT):
                    chain.mark(nc.vector.bn_aggr(mv[:, j], stats[:, j]))
                chain.wait()
                nc.vector.tensor_scalar(var[:], mv[:, :, 1], EPS, None, ALU.add).then_inc(s_var, 1)

            def normalise(n):
                dve.wait_ge(s_rstd, n + 1)
                if n:
                    dve.wait_ge(s_t, n)
                for j in range(NT):
                    last = nc.vector.tensor_scalar(xn[:, j], xs[:, n % 2, j], mv[:, j, 0:1], rstd[:, j:j + 1],
                                                   ALU.subtract, ALU.mult)
                last.then_inc(s_xn, 1)

            def rest_of(n, a):
                rows = rows_of(a)
                if n:
                    dve.wait_ge(s_lo[kind(a)], before(n, a))
                dve.wait_ge(s_hi[kind(a)], upto(n, a))
                nc.vector.tensor_tensor(rest[0:rows, a], whole(a), parts[0:rows, a, 0],
                                        ALU.subtract).then_inc(s_rest[kind(a)], 1)

            def rope(n, a):
                cols = slice((n % 2) * BANK, (n % 2 + 1) * BANK)
                dve.wait_ge(s_mm[0], NHEAD * n + 2 * a + 2)
                if n:
                    dve.wait_ge(s_rot, 2 * n - 1 + a)
                nc.vector.tensor_tensor(by_cos[:, a], ps[:, 1 + 2 * a], cos[:, cols], ALU.mult)
                nc.vector.tensor_tensor(by_sin[:, a], ps[:, 2 + 2 * a], sin[:, cols], ALU.mult).then_inc(s_rc, 1)

            def take_peaks(n):
                dve.wait_ge(s_nm, n + 1)
                if n:
                    dve.wait_ge(s_peak, n)
                nc.vector.tensor_tensor(peak[:], ps[:, 3, 0:2 * NT * HEADS], peak[:], ALU.max).then_inc(s_peak, 1)

            chain.link(nc.vector.memset(peak[:], 0.0))
            moments(0)
            normalise(0)
            for m in range(NA + 1):
                if m + 1 < NA:
                    moments(m + 1)
                if m == 0:
                    nc.vector.memset(q_op[64:KC], 0.0).then_inc(s_init, 1)
                if m < NA:
                    rest_of(m, 2)
                    rest_of(m, 3)
                fill(m, 0)
                if m + 1 < NA:
                    normalise(m + 1)
                if m < NA:
                    rest_of(m, 4)
                fill(m, 1)
                if m:
                    if m == 1:
                        dve.wait_ge(s_tab, 64)
                    rope(m - 1, 0)
                    rope(m - 1, 1)
                fill(m, 2)
                if m:
                    rest_of(m - 1, 0)
                    rest_of(m - 1, 1)
                    take_peaks(m - 1)
                fill(m, 3)
            dve.wait_ge(s_peak, NA)
            nc.vector.tensor_reduce(peak2[:], peak[:].rearrange("p (a j h) -> p a h j", a=2, j=NT), AX.X,
                                    ALU.max).then_inc(s_pk, 1)
            dve.wait_ge(s_pt, 1)
            chain.link(nc.vector.tensor_reduce(peak_t[:], ps[0:HEADS, 1, 0:2 * P].rearrange("h (a t) -> h a t", a=2),
                                               AX.X, ALU.max))
            nc.vector.tensor_tensor(peak_product[:], peak_t[:, 0:1], peak_t[:, 1:2], ALU.mult).then_inc(s_pk, 1)
            chain.link(nc.vector.memset(bound["row"][:], 0.0))
            chain.link(nc.vector.memset(bound["value"][:, 1:2], 0.5))
            dve.wait_ge(s_hb, 1)
            nc.vector.tensor_reduce(bound["value"][:, 0:1], ps[0:1, 2, 0:HEADS], AX.X, ALU.max).then_inc(s_sqb, 1)
            dve.wait_ge(s_sqb, 1)
            chain.link(nc.vector.tensor_scalar(bound["exact"][:], bound["value"][:, 0:1],
                                               (SAFE / LOGIT_SCALE) ** 2, None, ALU.is_gt))
            dve.wait_ge(s_root, 1)
            chain.link(nc.vector.tensor_scalar(bound["value"][:, 3:4], bound["value"][:, 2:3], -1.01, None, ALU.mult))
            chain.link(nc.vector.tensor_scalar(bound["row"][:], bound["row"][:], bound["value"][:, 3:4], None, ALU.add))

        @block.scalar
        def _(act):
            def fill(m, q):
                if slot(m, q) is not None:
                    if slot(m, q) == 0:
                        act.wait_ge(s_v, 2 * FIRST)
                    for c in FIRST_CHUNKS[slot(m, q)]:
                        sel.keep_positive(act, 0, c)

            def turned(n):
                if n >= 3:
                    act.wait_ge(s_mm[0], NHEAD * (n - 2))
                    act.wait_ge(s_mm[1], NINDEX * (n - 2))
                act.wait_ge(s_t, n + 1)
                nc.scalar.copy(xT[:, n % 3], ps[:, 0]).then_inc(s_xT, 1)

            def high(n, a):
                if n:
                    act.wait_ge(s_st[kind(a)], 16 * before(n, a))
                if a < 2:
                    act.wait_ge(s_rot, 2 * n + a + 1)
                else:
                    act.wait_ge(s_mm[1], NINDEX * n + MADE[SPLIT[a]])
                nc.scalar.copy(parts[0:rows_of(a), a, 0], whole(a)).then_inc(s_hi[kind(a)], 1)

            def middle(n, a):
                act.wait_ge(s_rest[kind(a)], upto(n, a))
                nc.scalar.copy(parts[0:rows_of(a), a, 1], rest[0:rows_of(a), a]).then_inc(s_mid[kind(a)], 1)

            def values(n, e):
                act.wait_ge(s_mm[1], NINDEX * n + 3 + e)
                src = ps[:, 1 + e, 0:2 * (P + IH)].rearrange("p (j c) -> p j c", j=2)
                tile = NT * n + 2 * e
                nc.scalar.copy(v_all[:, tile:tile + 2, :], src[:, :, 0:P])
                nc.scalar.copy(iw_all[:, tile:tile + 2, :], src[:, :, P:P + IH]).then_inc(s_v, 1)

            def square(n, a):
                if n:
                    act.wait_ge(s_nm, n)
                nc.scalar.activation(squares[:, a], rot[:, a], ACT.Square).then_inc(s_sq, 1)

            turned(0)
            for m in range(NA + 1):
                if m < NA:
                    high(m, 2)
                    high(m, 3)
                    values(m, 0)
                    values(m, 1)
                    middle(m, 2)
                    middle(m, 3)
                fill(m, 0)
                if m < NA:
                    high(m, 4)
                if m + 1 < NA:
                    turned(m + 1)
                if m < NA:
                    middle(m, 4)
                fill(m, 1)
                if m:
                    for a in range(2):
                        high(m - 1, a)
                        square(m - 1, a)
                fill(m, 2)
                if m:
                    middle(m - 1, 0)
                    middle(m - 1, 1)
                fill(m, 3)

        @block.gpsimd
        def _(pool):
            chain = Chain(pool, s_chp)

            def fill(m, q):
                if slot(m, q) is not None:
                    for c in FIRST_CHUNKS[slot(m, q)]:
                        sel.combine(pool, chain, 0, c)

            def rstd_of(n):
                pool.wait_ge(s_var, n + 1)
                if n:
                    pool.wait_ge(s_xn, n)
                nc.gpsimd.tensor_tensor(rstd[:], var[:], power[:], ALU.pow).then_inc(s_rstd, 1)

            def low(n, a):
                rows = rows_of(a)
                pool.wait_ge(s_mid[kind(a)], upto(n, a))
                nc.gpsimd.tensor_tensor(parts[0:rows, a, 2], rest[0:rows, a], parts[0:rows, a, 1],
                                        ALU.subtract).then_inc(s_lo[kind(a)], 1)

            def rotate(n, a):
                if n:
                    pool.wait_ge(s_rest[0], 2 * n)
                    pool.wait_ge(s_hi[0], 2 * n)
                    pool.wait_ge(s_sq, 2 * n)
                pool.wait_ge(s_rc, 2 * n + a + 1)
                nc.gpsimd.tensor_tensor(rot[:, a], by_cos[:, a], by_sin[:, a], ALU.add).then_inc(s_rot, 1)

            nc.gpsimd.memset(power[:], -0.5).then_inc(s_pow, 1)
            pool.wait_ge(s_pow, 1)
            rstd_of(0)
            for m in range(NA + 1):
                if m + 1 < NA:
                    rstd_of(m + 1)
                if m == 0:
                    pool.wait_ge(s_rstd, 2)
                    nc.gpsimd.memset(k_op[64:KC], 1.0).then_inc(s_init, 1)
                    pool.wait_ge(s_init, 2)
                if m < NA:
                    low(m, 2)
                    low(m, 3)
                fill(m, 0)
                if m < NA:
                    low(m, 4)
                fill(m, 1)
                if m:
                    rotate(m - 1, 0)
                    rotate(m - 1, 1)
                fill(m, 2)
                if m:
                    low(m - 1, 0)
                    low(m - 1, 1)
                fill(m, 3)
            pool.wait_ge(s_sqb, 1)
            nc.gpsimd.tensor_tensor(bound["value"][:, 2:3], bound["value"][:, 0:1], bound["value"][:, 1:2],
                                    ALU.pow).then_inc(s_root, 1)

        @block.tensor
        def _(pe):
            def fill(m, q):
                if slot(m, q) is not None:
                    for c in FIRST_CHUNKS[slot(m, q)]:
                        sel.dots(pe, 0, c)

            def turn(n):
                if n:
                    pe.wait_ge(s_rest[1], 3 * (n - 1) + 2)
                pe.wait_ge(s_xn, n + 1)
                for j in range(NT):
                    last = nc.tensor.transpose(ps[:, 0, P * j:P * (j + 1)], xn[:, j], ident[:])
                last.then_inc(s_t, 1)

            def product(n, name, bank, phase, rows=P):
                nc.tensor.matmul(ps[0:rows, bank], w[:, COL[name]:COL[name] + rows], xT[:, n % 3],
                                 start=True, stop=True).then_inc(s_mm[phase], 1)

            def index_phase(n):
                pe.wait_ge(s_xT, n + 1)
                if n:
                    pe.wait_ge(s_rest[1], 3 * n)
                product(n, "iq0", 5, 1)
                product(n, "iq1", 0, 1)
                if n >= 2:
                    pe.wait_ge(s_rc, 2 * n - 3)
                if n:
                    pe.wait_ge(s_v, 2 * n)
                for e in range(2):
                    for j in range(2):
                        tile = 2 * e + j
                        last = nc.tensor.matmul(ps[:, 1 + e, (P + IH) * j:(P + IH) * (j + 1)],
                                                xT[:, n % 3, P * tile:P * (tile + 1)],
                                                w[:, COL["v"]:COL["v"] + P + IH], start=True, stop=True)
                    last.then_inc(s_mm[1], 1)

            def last_key(n):
                pe.wait_ge(s_rest[1], 3 * n + 1)
                product(n, "ik", 5, 1, ID)

            def head_phase(n):
                pe.wait_ge(s_v, min(2 * n + 4, 2 * NA))
                product(n, "q", 1, 0)
                product(n, "qs", 2, 0)
                if n:
                    pe.wait_ge(s_peak, n)
                    pe.wait_ge(s_rc, 2 * n)
                product(n, "k", 3, 0)
                product(n, "ks", 4, 0)

            def norms(n):
                pe.wait_ge(s_rc, 2 * n + 2)
                pe.wait_ge(s_sq, 2 * n + 2)
                for m in range(2 * NT):
                    last = nc.tensor.matmul(ps[:, 3, HEADS * m:HEADS * (m + 1)],
                                            squares[:, m // NT, P * (m % NT):P * (m % NT + 1)], head_of[:],
                                            start=True, stop=True)
                last.then_inc(s_nm, 1)

            pe.wait_ge(s_id, 16)
            turn(0)
            pe.wait_ge(s_w, 16)
            for m in range(NA + 1):
                if m < NA:
                    index_phase(m)
                fill(m, 0)
                if m < NA:
                    last_key(m)
                if m + 1 < NA:
                    turn(m + 1)
                fill(m, 1)
                if m:
                    head_phase(m - 1)
                fill(m, 2)
                if m:
                    if m == 1:
                        pe.wait_ge(s_tab, 64)
                    norms(m - 1)
                fill(m, 3)
            pe.wait_ge(s_pk, 1)
            pe.wait_ge(s_v, 2 * NA)
            for a in range(2):
                last = nc.tensor.transpose(ps[0:HEADS, 1, P * a:P * (a + 1)], peak2[:, a], ident[:])
            last.then_inc(s_pt, 1)
            pe.wait_ge(s_pk, 2)
            nc.tensor.matmul(ps[0:1, 2, 0:HEADS], peak_product[:], ident[0:HEADS, 0:HEADS], start=True,
                             stop=True).then_inc(s_hb, 1)


def attend_all(nc, t, ident, identb, sel, v_all, q_op, k_op, bound, s_qk, ffn):
    with ExitStack() as ctx:
        def sb(name, shape, dt):
            return ctx.enter_context(nc.sbuf_tensor(name, shape, dt))

        def sem(name):
            return ctx.enter_context(nc.semaphore(name))

        NMAX = (TILES // GROUPS) * HL
        NCL = 16 * PARTS * HL
        v_op = sb("v_op", [P, TILES, HEADS, VW], F32)
        hidden = sel.hidden
        hidden_t = sb("hidden_t", [P, TILES, S], BF16)
        probs = sb("probs", [P, PB, HL, BANK], F32)
        out_t = sb("out_t", [P, 2, BANK], F32)
        recip = sb("recip", [P, 4, HL], F32)
        rows_out = sb("rows_out", [P, TILES, D], F32)
        top = sb("top", [P, NMAX], F32)
        neg = sb("neg", [NMAX, 3, P], F32)
        neg_parts = sb("neg_parts", [NMAX, PARTS, P], BF16)

        ps_s = ctx.enter_context(nc.psum_tensor("ps_s", [P, 4, BANK], F32))
        ps_o = ctx.enter_context(nc.psum_tensor("ps_o", [P, BANK], F32))
        ps_d = sel.dots_ps
        ps_t = ctx.enter_context(nc.psum_tensor("ps_t", [P, BANK], F32))
        pair_banks = [ps_s[:, 0:2], ps_s[:, 2:4], ps_d[:, 0:2]]
        turn_bank = ps_t[:].bitcast(BF16)

        def turned(v):
            at = 0
            for j, lo, hi in turned_blocks(v):
                yield hidden_t[:, j, P * lo:P * hi], turn_bank[:, at:at + P * (hi - lo)]
                at += P * (hi - lo)

        def wait_turned(eng, b, v):
            eng.wait_ge(s_hid[v % 2], NTURN // 2 * b + v // 2 + 1)

        s_relu, s_sel = sel.s_relu, sel.s_sel
        s_fill = sem("value_operand_filled")
        s_turned = sem("selection_turned")
        s_hid = [sem("hidden_t_even_ready"), sem("hidden_t_odd_ready")]
        s_v = sem("values_placed")
        s_sc = sem("logits_ready")
        s_p = sem("probs_ready")
        s_pv = sem("pv_done")
        s_mask = sem("weights_masked")
        s_oc = sem("out_copied")
        s_ot = sem("out_turned")
        s_norm = sem("normalised")
        s_ms = sem("max_logits_ready")
        s_mt = sem("max_taken")
        s_mtop = sem("maxima_ready")
        s_mturn = sem("maxima_turned")
        s_neg = sem("neg_parts_ready")
        s_cl = sem("max_rows_loaded")
        s_st = sem("rows_stored")
        s_chv = sem("vector_chain")
        s_chp = sem("pool_chain")
        s_cht = sem("selection_chain")
        s_chm = sem("maxima_chain")
        block = ctx.enter_context(nc.Block())

        @block.sync
        def _(sp):
            def load_maxima(b, hg, g):
                sp.wait_ge(s_neg, NGRP * b + GROUPS * hg + g + 1)
                for p in range(PARTS):
                    for hl in range(HL):
                        dst = q_op[KROWS + p:KROWS + p + 1, hg % 2, hl, BANK * g:BANK * (g + 1)]
                        sp.dma_start(dst.rearrange("o (i t) -> o i t", i=TILES // GROUPS),
                                     neg_parts[4 * hl:4 * hl + 4, p, :]).then_inc(s_cl, 16)

            src = bound["row"][:].rearrange("o (n t) -> o n t", n=1).broadcast_to([1, HL * S // BANK, BANK])
            for r in range(2):
                sp.dma_start(q_op[KROWS:KROWS + 1, r].rearrange("o h (n t) -> o (h n) t", t=BANK), src)\
                  .then_inc(s_cl, 16)
            exact = sp.value_load(bound["exact"][0:1, 0:1], min_val=0, max_val=1)

            sp.wait_ge(s_cl, 32)

            def next_index(b):
                sp.wait_ge(sel.s_dots, NCHUNK * b)
                sel.load(sp, t, b)

            def batch(b, more, index):
                for hg in range(HG):
                    with sp.If(exact > 0):
                        for g in range(GROUPS):
                            load_maxima(b, hg, g)
                    if hg + 2 < HG or more:
                        sp.wait_ge(s_sc, NPAIR * b + (NPAIR // HG) * (hg + 1))
                        load_head_group(sp, t, q_op, k_op, s_qk, b + (hg + 2) // HG, (hg + 2) % HG)
                    if hg == 2 and index:
                        next_index(b + 2)

            with sp.Fori(0, B - 2) as b:
                batch(b, True, True)
            batch(B - 2, True, False)
            ffn.load_weights(sp, t)
            sp.wait_ge(s_st, 16)
            for half in range(2):
                ffn.load_rows(sp, t, 0, half)
            batch(B - 1, False, False)
            sp.wait_ge(s_st, 16 * B)

        @block.tensor
        def _(pe):
            def turn_selection(b, v, normalised):
                pe.wait_ge(s_sel, TILES * b + (TILES // 2 if v < 2 else TILES))
                pe.wait_ge(s_norm, normalised)
                if v:
                    wait_turned(pe, b, v - 1)
                else:
                    pe.wait_ge(s_hid[1], NTURN // 2 * b)
                at = 0
                for j, lo, hi in turned_blocks(v):
                    for i in range(lo, hi):
                        last = nc.tensor.transpose(turn_bank[:, at:at + P], hidden[:, i, P * j:P * (j + 1)], identb[:])
                        at += P
                last.then_inc(s_turned, 1)

            def row_maxima(b, hg, g):
                r = hg % 2
                n = GROUPS * hg + g
                first = NMAX * (NGRP * b + n)
                pe.wait_ge(s_p, NPAIR * b + 2 * (GROUP_END[n - 1] + 1 if n else 0))
                wait_turned(pe, b, 4 if g else 0)
                wait_turned(pe, b, 5 if g else 1)
                for m in range(NMAX):
                    i, hl = 4 * g + m // HL, m % HL
                    if m >= 2:
                        pe.wait_ge(s_mt, first + m - 1)
                    for c0 in range(0, P * (i + 1), BANK):
                        wd = min(BANK, P * (i + 1) - c0)
                        bank = ps_s[:, 2 * (m % 2) + c0 // BANK, 0:wd]
                        nc.tensor.matmul(bank, q_op[0:KROWS, r, hl, P * i:P * (i + 1)],
                                         k_op[0:KROWS, r, hl, c0:c0 + wd], start=True, stop=False,
                                         skip_group_check=True)
                        for j in range(c0 // P, (c0 + wd) // P):
                            last = nc.tensor.matmul(bank[:, P * j - c0:P * j - c0 + P],
                                                    hidden_t[:, j, P * i:P * (i + 1)], identb[:],
                                                    start=False, stop=(P * (j + 1) == c0 + wd),
                                                    skip_group_check=True)
                    last.then_inc(s_ms, 1)
                pe.wait_ge(s_mtop, NGRP * b + n + 1)
                nc.tensor.transpose(ps_s[0:NMAX, 0, 0:P], top[:], ident[:]).then_inc(s_mturn, 1)
                pe.wait_ge(s_cl, 32 + NCL * (NGRP * b + n + 1))

            def logits(b, k, hidden_heads=HL, banks=2):
                hg, g, j = STEPS[k]
                r = hg % 2
                t0, wd = span(k)
                if hg == 0:
                    wait_turned(pe, b, 2 * g + j // 2)
                for p in range(2):
                    pair = pair_banks[(2 * k + p) % banks]
                    pe.wait_ge(s_p, NPAIR * b + max(2 * k + p + 1 - banks, 0))
                    for e in range(2):
                        if 2 * p + e < hidden_heads:
                            nc.tensor.matmul(pair[:, e, 0:wd], identb[:], hidden_t[:, j, t0:t0 + wd],
                                             start=True, stop=False)
                    for e in range(2):
                        last = nc.tensor.matmul(pair[:, e, 0:wd], k_op[:, r, 2 * p + e, P * j:P * (j + 1)],
                                                q_op[:, r, 2 * p + e, t0:t0 + wd],
                                                start=(2 * p + e >= hidden_heads), stop=True)
                    last.then_inc(s_sc, 1)

            def weigh(b, k, masked=False):
                hg, g, j = STEPS[k]
                t0, wd = span(k)
                n = GROUPS * hg + g
                if k == 0:
                    pe.wait_ge(s_v, b + 1)
                if j == 0 and not (isinstance(b, int) and b == 0 and n == 0):
                    pe.wait_ge(s_oc, NGRP * b + n)
                pe.wait_ge(s_p, NPAIR * b + 2 * k + 2)
                if masked:
                    pe.wait_ge(s_mask, 2 * k + 2)
                for hl in range(HL):
                    last = nc.tensor.matmul(ps_o[VW * hl:VW * (hl + 1), t0 - BANK * g:BANK],
                                            v_op[:, j, HL * hg + hl, :], probs[:, k % PB, hl, 0:wd],
                                            start=(j == 0), stop=(k in GROUP_END))
                last.then_inc(s_pv, 1)

            def turn_out(b, n, more=False):
                pe.wait_ge(s_oc, NGRP * b + n + 1)
                if n:
                    pe.wait_ge(s_norm, NGRP * b + n)
                if n == 0:
                    wait_turned(pe, b, NTURN - 1)
                if n == NGRP - 1 and more:
                    wait_turned(pe, b + 1, 1)
                for c in range(4):
                    last = nc.tensor.transpose(ps_t[:, P * c:P * (c + 1)], out_t[:, n % 2, P * c:P * (c + 1)],
                                               ident[:])
                last.then_inc(s_ot, 1)

            def load_done(b, hg):
                pe.wait_ge(s_qk[hg % 2], 16 * QK_DMAS * (2 * b + hg // 2 + 1))

            def begin(b, k):
                hg, g, j = STEPS[k]
                if j == 0:
                    load_done(b, hg)
                    with pe.If(exact > 0):
                        row_maxima(b, hg, g)
                logits(b, k)

            def batch(b):
                begin(b, 0)
                for k in range(NSTEP):
                    if k + 1 < NSTEP:
                        begin(b, k + 1)
                    if k in TURNS:
                        turn_selection(b, TURNS[k][0], NGRP * b)
                    weigh(b, k)
                    if k in TURNS:
                        turn_selection(b, TURNS[k][1], NGRP * b)
                    if k - 1 in GROUP_END:
                        turn_out(b, GROUP_END.index(k - 1))
                    for c in EARLY_AT.get(k, []):
                        sel.dots(pe, b + 1, c)
                    for c in CHUNKS_AT[k]:
                        sel.dots(pe, b + 1, c)
                    if k in NEXT_TURNS:
                        turn_selection(b + 1, NEXT_TURNS[k], NGRP * b + NGRP - 1)
                turn_out(b, NGRP - 1, True)

            def last_batch(b, exact_maxima):
                def begin_last(k):
                    hg, g, j = STEPS[k]
                    if j == 0:
                        load_done(b, hg)
                        if exact_maxima:
                            row_maxima(b, hg, g)
                    logits(b, k, HL if exact_maxima else UNMASKED, banks=3)

                begin_last(0)
                begin_last(1)
                for k in range(NSTEP):
                    if k + 2 < NSTEP:
                        begin_last(k + 2)
                    if k in TURNS:
                        turn_selection(b, TURNS[k][0], NGRP * b)
                    weigh(b, k, masked=True)
                    if k in TURNS:
                        turn_selection(b, TURNS[k][1], NGRP * b)
                    if k - 1 in GROUP_END:
                        turn_out(b, GROUP_END.index(k - 1))
                turn_out(b, NGRP - 1)

            for v in range(2):
                turn_selection(0, v, 0)
            pe.wait_ge(s_cl, 32)
            exact = pe.value_load(bound["exact"][0:1, 0:1], min_val=0, max_val=1)
            with pe.Fori(0, B - 1) as b:
                batch(b)
            with pe.If(exact > 0):
                last_batch(B - 1, True)
            with pe.If(exact < 1):
                last_batch(B - 1, False)

        @block.scalar
        def _(act):
            def exponents(b, k, banks=2):
                t0, wd = span(k)
                act.wait_ge(s_pv, NSTEP * b + max(k - PB + 1, 0))
                for p in range(2):
                    act.wait_ge(s_sc, NPAIR * b + 2 * k + p + 1)
                    nc.scalar.activation(probs[:, k % PB, 2 * p:2 * p + 2, 0:wd],
                                         pair_banks[(2 * k + p) % banks][:, :, 0:wd],
                                         ACT.Exp, scale=LOGIT_SCALE).then_inc(s_p, 1)

            def copy_out(b, n):
                act.wait_ge(s_pv, NSTEP * b + GROUP_END[n] + 1)
                act.wait_ge(s_ot, NGRP * b + max(n - 1, 0))
                nc.scalar.copy(out_t[:, n % 2], ps_o[:]).then_inc(s_oc, 1)

            def take_turned(b, v):
                act.wait_ge(s_turned, NTURN * b + v + 1)
                for dst, src in turned(v):
                    last = nc.scalar.copy(dst, src)
                last.then_inc(s_hid[1], 1)

            def batch(b):
                exponents(b, 0)
                for k in range(NSTEP):
                    if k + 1 < NSTEP:
                        exponents(b, k + 1)
                    if k in TURNS:
                        take_turned(b, TURNS[k][1])
                    if k in GROUP_END:
                        copy_out(b, GROUP_END.index(k))
                    for c in EARLY_AT.get(k, []):
                        sel.keep_positive(act, b + 1, c)
                    for c in CHUNKS_AT[k]:
                        sel.keep_positive(act, b + 1, c)
                    if NEXT_TURNS.get(k) == 1:
                        take_turned(b + 1, 1)

            take_turned(0, 1)
            with act.Fori(0, B - 1) as b:
                batch(b)
            exponents(B - 1, 0, 3)
            exponents(B - 1, 1, 3)
            for k in range(NSTEP):
                if k + 2 < NSTEP:
                    exponents(B - 1, k + 2, 3)
                if k in TURNS:
                    take_turned(B - 1, TURNS[k][1])
                if k in GROUP_END:
                    copy_out(B - 1, GROUP_END.index(k))

        @block.gpsimd
        def _(pool):
            chain = Chain(pool, s_chp)
            chain.link(nc.gpsimd.memset(v_op[:, :, :, DK:VW], 0.0))
            nc.gpsimd.memset(v_op[:, :, :, DK:DK + 1], 1.0).then_inc(s_fill, 1)
            pool.wait_ge(s_fill, 1)

            def place_values(b):
                pool.wait_ge(s_pv, NSTEP * b)
                nc.gpsimd.tensor_copy(v_op[:, :, :, 0:DK],
                                      v_all[:, bass.ds(TILES * b, TILES), :].rearrange("p j (h d) -> p j h d", h=HEADS)
                                      ).then_inc(s_v, 1)

            def store(b):
                pool.wait_ge(s_norm, NGRP * b + NGRP)
                pool.dma_start(t["rows"][b], rows_out[:]).then_inc(s_st, 16)

            place_values(0)
            with pool.Fori(0, B - 1) as b:
                sel.begin_combine(chain, b + 1)
                for c in range(NCHUNK):
                    sel.combine(pool, chain, b + 1, c)
                place_values(b + 1)
                store(b)
            store(B - 1)

        @block.vector
        def _(dve):
            chain = Chain(dve, s_chv)
            picks = Chain(dve, s_cht)
            exact_chain = Chain(dve, s_chm)

            def take_turned(b, v):
                dve.wait_ge(s_turned, NTURN * b + v + 1)
                for dst, src in turned(v):
                    last = nc.vector.tensor_copy(dst, src)
                last.then_inc(s_hid[0], 1)

            def maxima(b, n):
                exact_chain.restart()
                for m in range(NMAX):
                    i, hl = 4 * (n % GROUPS) + m // HL, m % HL
                    dve.wait_ge(s_ms, NMAX * (NGRP * b + n) + m + 1)
                    src = ps_s[:, 2 * (m % 2):2 * (m % 2) + 2].rearrange("p c t -> p (c t)")[:, 0:P * (i + 1)]
                    nc.vector.tensor_reduce(top[:, 4 * hl + i % 4:4 * hl + i % 4 + 1], src, AX.X,
                                            ALU.max).then_inc(s_mt, 1)
                dve.wait_ge(s_mt, NMAX * (NGRP * b + n + 1))
                dve.sem_inc(s_mtop, 1)
                dve.wait_ge(s_mturn, NGRP * b + n + 1)
                if n or not isinstance(b, int):
                    dve.wait_ge(s_cl, 32 + NCL * (NGRP * b + n))
                exact_chain.link(nc.vector.tensor_scalar(neg[:, 0], ps_s[0:NMAX, 0, 0:P], -1.0, None, ALU.mult))
                exact_chain.link(nc.vector.tensor_copy(neg_parts[:, 0], neg[:, 0]))
                exact_chain.link(nc.vector.tensor_tensor(neg[:, 1], neg[:, 0], neg_parts[:, 0], ALU.subtract))
                exact_chain.link(nc.vector.tensor_copy(neg_parts[:, 1], neg[:, 1]))
                nc.vector.tensor_tensor(neg_parts[:, 2], neg[:, 1], neg_parts[:, 1],
                                        ALU.subtract).then_inc(s_neg, 1)

            def normalise(b, n):
                hg, g = n // GROUPS, n % GROUPS
                dve.wait_ge(s_ot, NGRP * b + n + 1)
                if n == 0 and not (isinstance(b, int) and b == 0):
                    dve.wait_ge(s_st, 16 * b)
                src = ps_t[:].rearrange("p (c h v) -> p c h v", c=4, h=HL)
                chain.link(nc.vector.reciprocal(recip[:], src[:, :, :, DK]))
                dst = rows_out[:, 4 * g:4 * g + 4, 32 * hg:32 * hg + 32].rearrange("p c (h d) -> p c h d", h=HL)
                rb = recip[:].rearrange("p c (h o) -> p c h o", o=1).broadcast_to([P, 4, HL, DK])
                nc.vector.tensor_tensor(dst, src[:, :, :, 0:DK], rb, ALU.mult).then_inc(s_norm, 1)

            def batch(b):
                chain.restart()
                picks.restart()
                for p in range(PAIRS):
                    for r in range(ROUNDS + 1):
                        for what, n in EVENTS.get((p, r), []):
                            if what == "norm":
                                normalise(b, n)
                            elif what == "turn":
                                take_turned(b + 1, n)
                            else:
                                with dve.If(exact > 0):
                                    maxima(b, n)
                                if n == 0:
                                    for v in range(2, NTURN, 2):
                                        take_turned(b, v)
                        if r < ROUNDS:
                            sel.select(dve, picks, b + 1, p, r)

            def mask(b, k):
                hg, g, j = STEPS[k]
                t0, wd = span(k)
                for p, heads in ((1, slice(UNMASKED, 2)), (2, slice(2, HL))):
                    dve.wait_ge(s_p, NPAIR * b + 2 * k + p)
                    w = probs[:, k % PB, heads, 0:wd]
                    bias = hidden_t[:, j, t0:t0 + wd].rearrange("p (o t) -> p o t", o=1)
                    nc.vector.scalar_tensor_tensor(w, bias.broadcast_to([P, heads.stop - heads.start, wd]), -1.0, w,
                                                   ALU.is_ge, ALU.mult).then_inc(s_mask, 1)

            exact = dve.value_load(bound["exact"][0:1, 0:1], min_val=0, max_val=1)
            take_turned(0, 0)
            with dve.Fori(0, B - 1) as b:
                batch(b)
            chain.restart()
            for k in range(NSTEP):
                hg, g, j = STEPS[k]
                if j == 0:
                    with dve.If(exact > 0):
                        maxima(B - 1, GROUPS * hg + g)
                mask(B - 1, k)
                if k in TURNS:
                    take_turned(B - 1, TURNS[k][0])
                if k - 2 in GROUP_END:
                    normalise(B - 1, GROUP_END.index(k - 2))
            normalise(B - 1, NGRP - 1)


FFN_DMAS = 5


class FinishInputs:

    def __init__(self, nc, ctx):
        def sb(name, shape):
            return ctx.enter_context(nc.sbuf_tensor(name, shape, F32))

        self.NT, self.NH = BANK // P, STATE // P
        self.wo = sb("wo", [P, D])
        self.w1 = sb("w1", [P, STATE])
        self.w2 = sb("w2", [P, self.NH, D])
        self.b1 = sb("b1", [P, self.NH])
        self.b2 = sb("b2", [P, D])
        self.xs = sb("xf", [P, 2, self.NT, D])
        self.orow = sb("orow", [P, 2, self.NT, D])
        self.s_w = ctx.enter_context(nc.semaphore("ffn_weights_loaded"))
        self.s_x = [ctx.enter_context(nc.semaphore(f"rows_loaded{e}")) for e in range(2)]

    def load_rows(self, sp, t, b, half):
        rows = t["rows"][b, :, self.NT * half:self.NT * (half + 1)]
        sp.dma_start(self.orow[:, half], rows).then_inc(self.s_x[half], 16)
        sp.dma_start(self.xs[:, half], t["x"][b, half]).then_inc(self.s_x[half], 16)

    def load_weights(self, sp, t):
        for dst, name in ((self.wo, "wo"), (self.w1, "w1"), (self.b1, "b1"), (self.w2, "w2"), (self.b2, "b2")):
            sp.dma_start(dst[:], t[name]).then_inc(self.s_w, 16)


def finish_all(nc, t, ident, ffn):
    with ExitStack() as ctx:
        def sb(name, shape, dt):
            return ctx.enter_context(nc.sbuf_tensor(name, shape, dt))

        def sem(name):
            return ctx.enter_context(nc.semaphore(name))

        NT, NH = ffn.NT, ffn.NH
        wo, w1, w2, b1, b2, xs, orow, s_x, s_w = (ffn.wo, ffn.w1, ffn.w2, ffn.b1, ffn.b2, ffn.xs, ffn.orow, ffn.s_x,
                                                  ffn.s_w)
        oT = sb("oTf", [P, BANK], F32)
        x2 = sb("x2", [P, 2, NT, D], F32)
        stats = sb("statsf", [P, NT, 6], F32)
        mv = sb("mvf", [P, NT, 2], F32)
        var = sb("varf", [P, NT], F32)
        power = sb("powerf", [P, NT], F32)
        rstd = sb("rstdf", [P, NT], F32)
        xn = sb("xnf", [P, NT, D], F32)
        xT = sb("xTf", [P, BANK], F32)
        h = sb("h", [P, NH, BANK], F32)
        res = sb("res", [P, 2, NT, D], F32)
        ps = ctx.enter_context(nc.psum_tensor("psf", [P, 8, BANK], F32))

        s_ot = sem("attn_turned")
        s_oT = sem("attn_t_copied")
        s_pr = sem("attn_projected")
        s_x2 = sem("x2_ready")
        s_pow = sem("power2_filled")
        s_var = sem("variances2_ready")
        s_rstd = sem("rstd2_ready")
        s_xn = sem("xn2_ready")
        s_t = sem("xn2_turned")
        s_xT = sem("xn2_t_copied")
        s_h = sem("hidden_products")
        s_g = sem("gelu_done")
        s_y = sem("ffn_products")
        s_res = sem("result_ready")
        s_st = sem("result_stored")
        s_ch = sem("vector_chain_f")
        block = ctx.enter_context(nc.Block())

        @block.sync
        def _(sp):
            def batch(b, loads):
                for half in range(2):
                    n = 2 * b + half
                    if half < loads:
                        sp.wait_ge(s_x2, n + 2)
                        ffn.load_rows(sp, t, b + 1 + half, 1 - half)
                    sp.wait_ge(s_res, n + 1)
                    sp.dma_start(t["out"][b, half], res[:, half]).then_inc(s_st, 16)

            sp.wait_ge(s_x2, 1)
            ffn.load_rows(sp, t, 1, 0)
            with sp.Fori(0, B - 2) as b:
                batch(b, 2)
            batch(B - 2, 1)
            batch(B - 1, 0)
            sp.wait_ge(s_st, 16 * 2 * B)

        @block.tensor
        def _(pe):
            def turn_attn(b, half):
                n = 2 * b + half
                pe.wait_ge(s_x[half], 32 * b + 32)
                pe.wait_ge(s_oT, n)
                for j in range(NT):
                    last = nc.tensor.transpose(ps[:, 0, P * j:P * (j + 1)], orow[:, half, j], ident[:])
                last.then_inc(s_ot, 1)

            def project(n):
                pe.wait_ge(s_x2, n)
                pe.wait_ge(s_oT, n + 1)
                for j in range(NT):
                    last = nc.tensor.matmul(ps[:, 1, P * j:P * (j + 1)], oT[:, P * j:P * (j + 1)], wo[:],
                                            start=True, stop=True)
                last.then_inc(s_pr, 1)

            def turn_xn(n):
                pe.wait_ge(s_xT, n)
                pe.wait_ge(s_xn, n + 1)
                for j in range(NT):
                    last = nc.tensor.transpose(ps[:, 2, P * j:P * (j + 1)], xn[:, j], ident[:])
                last.then_inc(s_t, 1)

            def batch(b, more):
                for half in range(2):
                    n = 2 * b + half
                    pe.wait_ge(s_g, NH * n)
                    pe.wait_ge(s_xT, n + 1)
                    for m in range(NH):
                        nc.tensor.matmul(ps[:, 3 + m], w1[:, P * m:P * (m + 1)], xT[:], start=True,
                                         stop=True).then_inc(s_h, 1)
                    if more:
                        turn_attn(b + 1, half)
                    pe.wait_ge(s_res, n)
                    pe.wait_ge(s_g, NH * n + NH)
                    for j in range(NT):
                        for m in range(NH):
                            last = nc.tensor.matmul(ps[:, 7, P * j:P * (j + 1)], h[:, m, P * j:P * (j + 1)],
                                                    w2[:, m], start=(m == 0), stop=(m == NH - 1))
                    last.then_inc(s_y, 1)
                    if half == 0 or more:
                        turn_xn(n + 1)
                    if more:
                        project(n + 2)

            pe.wait_ge(s_w, 16 * FFN_DMAS)
            for half in range(2):
                turn_attn(0, half)
                project(half)
            turn_xn(0)
            with pe.Fori(0, B - 1) as b:
                batch(b, True)
            batch(B - 1, False)

        @block.scalar
        def _(act):
            def copy_attn(n):
                act.wait_ge(s_pr, n)
                act.wait_ge(s_ot, n + 1)
                nc.scalar.copy(oT[:], ps[:, 0]).then_inc(s_oT, 1)

            def copy_xn(n):
                act.wait_ge(s_h, NH * n)
                act.wait_ge(s_t, n + 1)
                nc.scalar.copy(xT[:], ps[:, 2]).then_inc(s_xT, 1)

            def batch(b, more):
                for half in range(2):
                    n = 2 * b + half
                    act.wait_ge(s_y, n)
                    for m in range(NH):
                        act.wait_ge(s_h, NH * n + m + 1)
                        nc.scalar.activation(h[:, m], ps[:, 3 + m], ACT.Gelu, bias=b1[:, m:m + 1]).then_inc(s_g, 1)
                    if more:
                        copy_attn(n + 2)
                    if half == 0 or more:
                        copy_xn(n + 1)

            act.wait_ge(s_w, 16 * FFN_DMAS)
            copy_attn(0)
            copy_attn(1)
            copy_xn(0)
            with act.Fori(0, B - 1) as b:
                batch(b, True)
            batch(B - 1, False)

        @block.gpsimd
        def _(pool):
            nc.gpsimd.memset(power[:], -0.5).then_inc(s_pow, 1)
            pool.wait_ge(s_pow, 1)
            with pool.Fori(0, 2 * B) as n:
                pool.wait_ge(s_var, n + 1)
                pool.wait_ge(s_xn, n)
                nc.gpsimd.tensor_tensor(rstd[:], var[:], power[:], ALU.pow).then_inc(s_rstd, 1)

        @block.vector
        def _(dve):
            chain = Chain(dve, s_ch)

            def residual_and_norm(b, half):
                n = 2 * b + half
                if not isinstance(n, int):
                    dve.wait_ge(s_res, n - 1)
                dve.wait_ge(s_x[half], 32 * b + 32)
                dve.wait_ge(s_pr, n + 1)
                nc.vector.tensor_tensor(x2[:, half].rearrange("p j d -> p (j d)"), ps[:, 1],
                                        xs[:, half].rearrange("p j d -> p (j d)"), ALU.add).then_inc(s_x2, 1)
                dve.wait_ge(s_x2, n + 1)
                for j in range(NT):
                    chain.mark(nc.vector.bn_stats(stats[:, j], x2[:, half, j]))
                chain.wait()
                for j in range(NT):
                    chain.mark(nc.vector.bn_aggr(mv[:, j], stats[:, j]))
                chain.wait()
                nc.vector.tensor_scalar(var[:], mv[:, :, 1], EPS, None, ALU.add).then_inc(s_var, 1)
                dve.wait_ge(s_rstd, n + 1)
                dve.wait_ge(s_t, n)
                for j in range(NT):
                    last = nc.vector.tensor_scalar(xn[:, j], x2[:, half, j], mv[:, j, 0:1], rstd[:, j:j + 1],
                                                   ALU.subtract, ALU.mult)
                last.then_inc(s_xn, 1)
                dve.wait_ge(s_xn, n + 1)
                b2v = b2[:].rearrange("p (o d) -> p o d", o=1).broadcast_to([P, NT, D])
                chain.link(nc.vector.tensor_tensor(x2[:, half], x2[:, half], b2v, ALU.add))

            def batch(b, more):
                chain.restart()
                for half in range(2):
                    n = 2 * b + half
                    dve.wait_ge(s_y, n + 1)
                    dve.wait_ge(s_st, 32 * b)
                    nc.vector.tensor_tensor(res[:, half].rearrange("p j d -> p (j d)"), ps[:, 7],
                                            x2[:, half].rearrange("p j d -> p (j d)"), ALU.add).then_inc(s_res, 1)
                    if more:
                        residual_and_norm(b + 1, half)

            dve.wait_ge(s_w, 16 * FFN_DMAS)
            residual_and_norm(0, 0)
            residual_and_norm(0, 1)
            with dve.Fori(0, B - 1) as b:
                batch(b, True)
            batch(B - 1, False)


def build(nc, t):
    with ExitStack() as ctx:
        ident = ctx.enter_context(nc.sbuf_tensor("ident", [P, P], F32))
        ffn = FinishInputs(nc, ctx)
        with ExitStack() as inner:
            def sb(name, shape, dt):
                return inner.enter_context(nc.sbuf_tensor(name, shape, dt))

            identb = sb("identb", [P, P], BF16)
            v_all = sb("v_all", [P, B * TILES, P], F32)
            iw_all = sb("iw_all", [P, B * TILES, IH], F32)
            q_op = sb("q_op", [KC, 2, HL, S], BF16)
            k_op = sb("k_op", [KC, 2, HL, S], BF16)
            bound = {"value": sb("bound", [1, 4], F32), "exact": sb("exact", [1, 1], mybir.dt.int32),
                     "row": sb("bound_row", [1, BANK], BF16)}
            s_init = inner.enter_context(nc.semaphore("operands_filled"))
            s_qk = [inner.enter_context(nc.semaphore(f"qk_loaded{r}")) for r in range(2)]
            sel = Selection(nc, inner, iw_all)
            project_and_select_first(nc, t, ident, identb, sel, v_all, iw_all, q_op, k_op, bound, s_init, s_qk)
            attend_all(nc, t, ident, identb, sel, v_all, q_op, k_op, bound, s_qk, ffn)
        finish_all(nc, t, ident, ffn)


def kernel(**inputs):
    import ml_dtypes
    import numpy as np
    import concourse.bacc as bacc
    from concourse.bass_utils import run_bass_kernel_spmd

    order = np.array([(hg * HL + hl) * DK + d for hg in range(HG) for d in range(DK) for hl in range(HL)])
    swap = order ^ 1
    qkv = np.asarray(inputs["L0_attn_qkv_w"])
    wq, wk, wv = qkv[0:D], qkv[D:2 * D], qkv[2 * D:3 * D]
    w = np.concatenate([wq[order], wq[swap], wk[order], wk[swap], np.asarray(inputs["L0_attn_iq_w"]),
                        np.asarray(inputs["L0_attn_ik_w"]), wv, np.asarray(inputs["L0_attn_iw_w"])], axis=0)
    w = np.ascontiguousarray(w.T)
    f32 = np.float32
    inv = (f32(1.0) / np.power(f32(1250.0), np.arange(0, DK, 2, dtype=f32) / f32(DK))).astype(f32)
    freqs = np.outer(np.arange(S, dtype=f32), inv).astype(f32)
    ch = order % DK
    cos = np.ascontiguousarray(np.cos(freqs)[:, ch // 2].T.astype(f32))
    sin = np.ascontiguousarray((np.sin(freqs)[:, ch // 2] * np.where(ch % 2 == 0, -1.0, 1.0)).T.astype(f32))
    eye = np.eye(P, dtype=f32)
    head_of = np.zeros((P, HEADS), ml_dtypes.bfloat16)
    head_of[np.arange(P), order // DK] = 1.0
    given = {
        "head_of": head_of,
        "x": np.asarray(inputs["L0_attn_x"]),
        "w": w, "cos": cos, "sin": sin, "ident": eye, "identb": eye.astype(ml_dtypes.bfloat16),
        "wo": np.ascontiguousarray(np.asarray(inputs["L0_attn_wo_w"]).T),
        "w1": np.asarray(inputs["L0_ffn_w1"]), "w2": np.asarray(inputs["L0_ffn_w2"]),
        "b1": np.asarray(inputs["L0_ffn_b1"]).reshape(STATE // P, P).T, "b2": np.asarray(inputs["L0_ffn_b2"]),
    }
    nc = bacc.Bacc("TRN2", target_bir_lowering=False, num_devices=1)
    t = {}
    arrays = {}
    for name, a in given.items():
        a = np.ascontiguousarray(a)
        arrays["in_" + name] = a
        t[name] = nc.dram_tensor("in_" + name, a.shape, mybir.dt.from_np(a.dtype), kind="ExternalInput").ap()
    NT = BANK // P
    t["x"] = t["x"].rearrange("b (g j p) d -> b g p j d", g=2, p=P)
    t["w2"] = t["w2"].rearrange("(m p) d -> p m d", p=P)
    t["b2"] = t["b2"].rearrange("(o d) -> o d", o=1).broadcast_to([P, D])
    t["iq_parts"] = nc.dram_tensor("iq_parts", (B, PARTS, IH, ID, S), BF16, kind="Internal").ap()
    for name in ("q", "k", "ik"):
        rows = ID if name == "ik" else P
        t[name + "_parts"] = nc.dram_tensor(name + "_parts", (B, PARTS, rows, S), BF16, kind="Internal").ap()
    t["rows"] = nc.dram_tensor("attn_rows", (B, P, TILES, D), F32, kind="Internal").ap()
    out = nc.dram_tensor("out_0", (B, S, D), F32, kind="ExternalOutput").ap()
    t["out"] = out.rearrange("b (g j p) d -> b g p j d", g=2, p=P)
    build(nc, t)
    r = run_bass_kernel_spmd(nc, [arrays], core_ids=[0])
    return r.results[0]["out_0"]
```
